# Optimizing a Trainium2 kernel written in Bass

```python
import numpy as np
import jax
import jax.numpy as jnp

def _softmax(x, axis=-1):
    return jax.nn.softmax(x, axis=axis)

def _gelu(x):
    return jax.nn.gelu(x, approximate=True)

def _silu(x):
    return jax.nn.silu(x)

def _sigmoid(x):
    return jax.nn.sigmoid(x)

def _layernorm(x, axis=-1, eps=1e-05):
    m = jnp.mean(x, axis=axis, keepdims=True)
    v = jnp.var(x, axis=axis, keepdims=True)
    return (x - m) / jnp.sqrt(v + eps)

def _scatter_add(tgt, idx, src, axis=0):
    return tgt.at[idx].add(src)

def _segment_sum(src, seg, n):
    return jax.ops.segment_sum(src, seg, n)
kernel_name = 'mk_prb_d1_jaxref_r4_4a2708'

def setup_inputs(seed: int=0):
    np.random.seed(seed)
    _w = jnp.asarray

    def _L0_attn_setup():
        import jax, jax.numpy as jnp
        import numpy as np
        B, S, D_MODEL, H, D = (2, 512, 256, 16, 64)
        SCALE = 1.0 / float(np.sqrt(D))

        def _rope(t, c, s):
            d2 = t.shape[-1] // 2
            t1, t2 = (t[..., :d2], t[..., d2:])
            return jnp.concatenate([t1 * c - t2 * s, t1 * s + t2 * c], axis=-1)
        key = jax.random.key(seed)
        ks = jax.random.split(key, 5)
        x = jax.random.normal(ks[0], (B, S, D_MODEL), jnp.float32)
        qkv_w = jax.random.normal(ks[1], (3 * H * D, D_MODEL), jnp.float32) * 0.02
        out_w = jax.random.normal(ks[2], (D_MODEL, H * D), jnp.float32) * 0.02
        bias_p = jax.random.uniform(ks[3], (H, 1, 1), jnp.float32) * 2.0
        bias_a = jax.random.uniform(ks[4], (H, 1, 1), jnp.float32)
        rope_freqs = 10000.0 ** (-jnp.arange(D // 2, dtype=jnp.float32) / (D // 2))
        return {'x': x, 'qkv_w': qkv_w, 'out_w': out_w, 'bias_p': bias_p, 'bias_a': bias_a, 'rope_freqs': rope_freqs}
    _L0_attn_in = _L0_attn_setup()

    def _L0_ffn_setup():
        import jax, jax.numpy as jnp
        import numpy as np
        key = jax.random.key(seed)
        k1, k2, k3, k4 = jax.random.split(key, 4)
        B, T, M = (4, 512, 256)
        E, F = (16, 1024)
        x = jax.random.normal(k1, (B, T, M), dtype=jnp.float32) * 0.02
        Wg = jax.random.normal(k2, (M, E), dtype=jnp.float32) * 0.02
        w1 = jax.random.normal(k3, (E, M, F), dtype=jnp.float32) * 0.02
        w2 = jax.random.normal(k4, (E, F, M), dtype=jnp.float32) * 0.02
        return {'x': x, 'Wg': Wg, 'w1': w1, 'w2': w2}
    _L0_ffn_in = _L0_ffn_setup()
    _d = {'L0_attn_x': _L0_attn_in['x'], 'L0_attn_qkv_w': _L0_attn_in['qkv_w'], 'L0_attn_out_w': _L0_attn_in['out_w'], 'L0_attn_bias_p': _L0_attn_in['bias_p'], 'L0_attn_bias_a': _L0_attn_in['bias_a'], 'L0_attn_rope_freqs': _L0_attn_in['rope_freqs'], 'L0_ffn_Wg': _L0_ffn_in['Wg'], 'L0_ffn_w1': _L0_ffn_in['w1'], 'L0_ffn_w2': _L0_ffn_in['w2']}
    _x0 = _d['L0_attn_x']
    _d['L0_attn_x'] = jax.random.normal(jax.random.fold_in(jax.random.key(seed), 1), (8, 512, 256), dtype=_x0.dtype)
    del _x0
    return _d

def reference(L0_attn_x, L0_attn_qkv_w, L0_attn_out_w, L0_attn_bias_p, L0_attn_bias_a, L0_attn_rope_freqs, L0_ffn_Wg, L0_ffn_w1, L0_ffn_w2):

    def _L0_attn_ref(x, qkv_w, out_w, bias_p, bias_a, rope_freqs):
        import jax, jax.numpy as jnp
        import numpy as np
        B, S, D_MODEL, H, D = (2, 512, 256, 16, 64)
        SCALE = 1.0 / float(np.sqrt(D))

        def _rope(t, c, s):
            d2 = t.shape[-1] // 2
            t1, t2 = (t[..., :d2], t[..., d2:])
            return jnp.concatenate([t1 * c - t2 * s, t1 * s + t2 * c], axis=-1)
        Bb, Ss, _ = x.shape
        qkv = (x @ qkv_w.T).reshape(Bb, Ss, 3, H, D)
        q = qkv[:, :, 0].transpose(0, 2, 1, 3)
        k = qkv[:, :, 1].transpose(0, 2, 1, 3)
        v = qkv[:, :, 2].transpose(0, 2, 1, 3)
        pos = jnp.arange(Ss, dtype=jnp.float32)
        ang = pos[:, None] * rope_freqs[None, :]
        c = jnp.cos(ang)[None, None]
        s = jnp.sin(ang)[None, None]
        q = _rope(q, c, s)
        k = _rope(k, c, s)
        scores = jnp.einsum('bhqd,bhkd->bhqk', q, k) * SCALE
        p = jnp.maximum(bias_p, 0.01)
        a = jnp.maximum(bias_a, 0.01)
        dist = jnp.abs(pos[None, :] - pos[:, None])
        kb = -p * jnp.log1p(a * dist)
        attn = jax.nn.softmax(scores + kb[None], axis=-1)
        out = jnp.einsum('bhqk,bhkd->bhqd', attn, v)
        out = out.transpose(0, 2, 1, 3).reshape(Bb, Ss, H * D)
        return out @ out_w.T

    def _L0_ffn_ref(x, Wg, w1, w2):
        import jax, jax.numpy as jnp
        import numpy as np
        d = x.shape[-1]
        xr = x.reshape(-1, d)
        S = xr.shape[0]
        E = Wg.shape[1]
        C = (S + E - 1) // E
        gate = jax.nn.softmax(xr @ Wg, axis=-1)
        idx = jnp.argmax(gate, axis=1)
        gates_s = jnp.take_along_axis(gate, idx[:, None], axis=1)[:, 0]
        onehot = jax.nn.one_hot(idx, E, dtype=jnp.int32)
        loc = jnp.sum((jnp.cumsum(onehot, axis=0) - 1) * onehot, axis=1)
        valid = loc < C
        loc_pad = jnp.minimum(loc, C)
        dispatched = jnp.zeros((E, C + 1, d), dtype=x.dtype).at[idx, loc_pad].set(xr)
        dispatched = dispatched[:, :C]
        h = jax.nn.relu(jnp.einsum('ecm,emf->ecf', dispatched, w1))
        expert_out = jnp.einsum('ecf,efm->ecm', h, w2)
        gathered = expert_out[idx, jnp.minimum(loc, C - 1)]
        combined = gathered * (gates_s * valid.astype(x.dtype))[:, None]
        return combined.reshape(x.shape)
    x = L0_attn_x
    xn = _layernorm(x, axis=-1)
    x = x + _L0_attn_ref(xn, L0_attn_qkv_w, L0_attn_out_w, L0_attn_bias_p, L0_attn_bias_a, L0_attn_rope_freqs) + _L0_ffn_ref(xn, L0_ffn_Wg, L0_ffn_w1, L0_ffn_w2)
    return x

_drawn_inputs = setup_inputs


def setup_inputs(seed=0):
    import zlib

    import numpy as np

    out = dict(_drawn_inputs(seed))
    spreads = {}
    factors = {'L0_attn_rope_freqs': 64.0,
     'L0_ffn_Wg': 3.836,
     'L0_ffn_w1': 4.492,
     'L0_ffn_w2': 3.725,
     'L0_attn_bias_p': 2.733,
     'L0_attn_bias_a': 3.211}
    for name, (base, spread) in spreads.items():
        noise = np.random.default_rng([zlib.crc32(name.encode()), seed]).standard_normal(out[name].shape)
        drawn = base * np.exp(spread * noise) if base else spread * noise
        out[name] = jnp.asarray(drawn.astype(out[name].dtype))
    for name, factor in factors.items():
        out[name] = (out[name] * factor).astype(out[name].dtype)
    return out
```

```python
from contextlib import ExitStack

import concourse.bass as bass
from concourse import mybir

F32 = mybir.dt.float32
F16 = mybir.dt.float16
I32 = mybir.dt.int32
U32 = mybir.dt.uint32
ALU = mybir.AluOpType
ACT = mybir.ActivationFunctionType
AX_X = mybir.AxisListType.X

P = 128
BANK = 512
NB, S, M = 8, 512, 256
H, D = 16, 64
E, F, C = 16, 1024, 256
TOK = NB * S
NT = TOK // P
TPB = S // P
KT = M // P
NG, HG = 4, 4
SW = S + (TPB - 1) * P
EPS = 1e-5
TWO_PI_PARTS = (6.28125, 0.0019340515136718750, 1.2554228305816650e-06, 3.8192e-10)
INV_TWO_PI = 0.15915494309189535
PI_BELOW = 3.1415925
ROUND = 12582912.0
P_SCALE = 16384.0
PAIRS = NG * HG * TPB // 2
FILLS = 6


def dve_linker(dve, sem):
    count = [0]

    def link(ins):
        count[0] += 1
        ins.then_inc(sem, 1)
        dve.wait_ge(sem, count[0])

    return link


def power_of_two(link, nc, n2, tmp, scale, inverse):
    link(nc.vector.tensor_scalar(tmp, n2.bitcast(I32), 23, None, ALU.logical_shift_right))
    link(nc.vector.tensor_scalar(tmp, tmp, 1, None, ALU.add))
    link(nc.vector.tensor_scalar(tmp, tmp, 1, None, ALU.logical_shift_right))
    link(nc.vector.tensor_scalar(tmp, tmp, -1, 201, ALU.mult, ALU.add))
    link(nc.vector.tensor_scalar(tmp, tmp, 167, None, ALU.min))
    link(nc.vector.tensor_scalar(scale.bitcast(I32), tmp, 23, None, ALU.logical_shift_left))
    link(nc.vector.tensor_scalar(tmp, tmp, -1, 254, ALU.mult, ALU.add))
    link(nc.vector.tensor_scalar(inverse.bitcast(I32), tmp, 23, None, ALU.logical_shift_left))


def layer(nc, x, qkv_w, out_w, bias_p, bias_a, rope_freqs, wg, w1, w2, out):
    x_tiles = x.rearrange("b (t p) m -> p (b t) m", p=P)
    xt_dram = nc.dram_tensor("xt_dram", (NB, P, 2 * KT * S), F16, kind="Internal").ap()
    slots_dram = nc.dram_tensor("slots_dram", (E * C, M), F32, kind="Internal").ap()
    expert_dram = nc.dram_tensor("expert_dram", (E * C, M), F32, kind="Internal").ap()
    base_dram = nc.dram_tensor("base_dram", (NB, P, TPB * M), F32, kind="Internal").ap()

    with ExitStack() as whole:
        def keep(name, shape, dt=F32):
            return whole.enter_context(nc.sbuf_tensor(name, shape, dt))

        def sem(name):
            return whole.enter_context(nc.semaphore(name))

        ident = keep("ident", [P, P])
        wt = [keep(f"wqkv_{n}", [P, KT, 3 * H * D], F16) for n in ("hi", "lo")]
        wot = [keep(f"wout_{n}", [P, H * D // P, M], F16) for n in ("hi", "lo")]
        cos = keep("cos", [P, S])
        sin = keep("sin", [P, S])
        scale = keep("scale", [P, 2])
        inverse = keep("inverse", [P, 2])
        score_scale = keep("score_scale", [P, 1])
        y_scale = keep("y_scale", [P, 1])
        coef = keep("coef", [P, H])
        slope = keep("slope", [P, H])
        scatter_to = keep("scatter_to", [P, NT], U32)
        gather_from = keep("gather_from", [P, NT], U32)
        gate = keep("gate", [P, NT])
        prepare(nc, sem, x_tiles, qkv_w, out_w, bias_p, bias_a, rope_freqs, wg, xt_dram, slots_dram,
                ident, wt, wot, cos, sin, scale, inverse, score_scale, y_scale, coef, slope,
                scatter_to, gather_from, gate)
        experts(nc, sem, x_tiles, w1, w2, slots_dram, expert_dram, base_dram, ident, gather_from, gate)
        attention(nc, sem, out, xt_dram, base_dram, ident, wt, wot, cos, sin, score_scale, y_scale, coef, slope)


def prepare(nc, sem, x_tiles, qkv_w, out_w, bias_p, bias_a, rope_freqs, wg, xt_dram, slots_dram,
            ident, wt, wot, cos, sin, scale, inverse, score_scale, y_scale, coef, slope,
            scatter_to, gather_from, gate):
    with ExitStack() as ctx:
        def sb(name, shape, dt=F32):
            return ctx.enter_context(nc.sbuf_tensor(name, shape, dt))

        wraw = sb("wraw", [P, 3 * H * D // P, M])
        wo_raw = sb("wo_raw", [P, KT, H * D])
        wg_sb = sb("wg_sb", [P, KT, E])
        xa = sb("xa", [P, NT, M])
        zeros = sb("zeros", [P, 2048])
        junk = sb("junk", [P, 2048])
        ones = sb("ones", [P, P])
        onesh = sb("onesh", [P, P], F16)
        before = sb("before", [P, P], F16)
        stats = sb("stats", [P, NT, 6])
        moments = sb("moments", [P, NT, 2])
        sd = sb("sd", [P, 4, NT])
        eps = sb("eps", [P, 1])
        freq = sb("freq", [P, 1])
        wsq = sb("wsq", [P, 4])
        n2 = sb("n2", [P, 2])
        expo = sb("expo", [P, 2], I32)
        pos = sb("pos", [P, S], I32)
        ang = sb("ang", [P, S])
        turns = sb("turns", [P, S])
        xt32 = sb("xt32", [P, 2, KT, S])
        xth = sb("xth", [P, 2, 2, KT, S], F16)
        iota_e = sb("iota_e", [P, NT, E], I32)
        lanes = sb("lanes", [P, NT, E])
        rt = sb("rt", [P, 6, NT * E])
        onehot = sb("onehot", [P, NT * E], F16)
        col = sb("col", [P, 8, NT])
        raw_p = sb("raw_p", [P, H])
        psx = [ctx.enter_context(nc.psum_tensor(f"psx{i}", [P, KT, S], F32)) for i in range(2)]
        psw = [ctx.enter_context(nc.psum_tensor(f"psw{i}", [P, BANK], F32)) for i in range(2)]
        psg = ctx.enter_context(nc.psum_tensor("psg", [P, BANK], F32))
        psn = ctx.enter_context(nc.psum_tensor("psn", [P, BANK], F32))

        ld_small, ld_w = sem("ld_small"), sem("ld_w")
        ld_x = [sem(f"ld_x{b}") for b in range(NB)]
        xt_stored = [sem(f"xt_stored{r}") for r in range(2)]
        const_ready, chain, pool_chain = sem("const_ready"), sem("chain_a"), sem("pool_chain_a")
        sq_done, n2_ready, scale_ready = sem("sq_done"), sem("n2_ready"), sem("scale_ready")
        var_ready, sd_ready, xn_ready = sem("var_ready"), sem("sd_ready"), sem("xn_ready")
        xt_ps, xt_hi, xt_lo, xt_32 = sem("xt_ps"), sem("xt_hi"), sem("xt_lo"), sem("xt_32")
        w_ps, w_hi, w_lo = sem("w_ps"), sem("w_hi"), sem("w_lo")
        logits_ready, shifted, exps = sem("logits_ready"), sem("shifted"), sem("exps")
        onehot_ready, counts_ready, routed = sem("onehot_ready"), sem("counts_ready"), sem("routed")
        ang_ready, sin_ready = sem("ang_ready"), sem("sin_ready")
        zero_ready, slots_zeroed, scattered = sem("zero_ready"), sem("slots_zeroed"), sem("scattered")
        NW = 3 * H * D // P * KT // 4
        NWO = H * D // P // 2
        logits = rt[:, 0, :].rearrange("p (t e) -> p t e", e=E)

        def r3(i):
            return rt[:, i, :].rearrange("p (t e) -> p t e", e=E)

        def spread(v):
            return v.unsqueeze(2).to_broadcast([P, NT, E])

        block = ctx.enter_context(nc.Block())

        @block.sync
        def _(sp):
            for b in range(NB):
                sp.dma_start(xa[:, b * TPB:(b + 1) * TPB, :], x_tiles[:, b * TPB:(b + 1) * TPB, :]).then_inc(ld_x[b], 16)
                if b == 0:
                    for q in range(4):
                        sp.dma_start(freq[32 * q:32 * q + 32, :], rope_freqs.unsqueeze(1)).then_inc(ld_small, 16)
                    sp.dma_start(wg_sb[:], wg.rearrange("(k p) e -> p k e", p=P)).then_inc(ld_small, 16)
                    sp.dma_start(slope[:], bias_a.rearrange("h a b -> (a b) h").to_broadcast([P, H])).then_inc(ld_small, 16)
                    sp.dma_start(raw_p[:], bias_p.rearrange("h a b -> (a b) h").to_broadcast([P, H])).then_inc(ld_small, 16)
            sp.dma_start(wraw[:], qkv_w.rearrange("(t p) m -> p t m", p=P)).then_inc(ld_w, 16)
            sp.dma_start(wo_raw[:], out_w.rearrange("(t p) n -> p t n", p=P)).then_inc(ld_w, 16)
            sp.wait_ge(zero_ready, 1)
            for q in range(4):
                rows = slots_dram[q * 1024:(q + 1) * 1024, :].rearrange("(p r) m -> p (r m)", p=P)
                sp.dma_start(rows, zeros[:]).then_inc(slots_zeroed, 16)
            for b in range(NB):
                sp.wait_ge(xt_lo, b + 1)
                sp.dma_start(xt_dram[b], xth[:, b % 2].rearrange("p h k s -> p (h k s)")).then_inc(xt_stored[b % 2], 16)
            for r in range(2):
                sp.wait_ge(xt_stored[r], 16 * (NB // 2))
            sp.wait_ge(slots_zeroed, 64)

        @block.gpsimd
        def _(pool):
            nc.gpsimd.memset(ones[:], 1.0).then_inc(pool_chain, 1)
            nc.gpsimd.memset(onesh[:], 1.0).then_inc(pool_chain, 1)
            nc.gpsimd.memset(ident[:], 0.0).then_inc(pool_chain, 1)
            pool.wait_ge(pool_chain, 3)
            nc.gpsimd.affine_select(out=ident[:], in_=ident[:], compare_op=ALU.not_equal, fill=1.0, base=0,
                                    pattern=[[-1, P]], channel_multiplier=1).then_inc(const_ready, 1)
            nc.gpsimd.affine_select(out=before[:], in_=onesh[:], compare_op=ALU.is_gt, fill=0.0, base=0,
                                    pattern=[[1, P]], channel_multiplier=-1).then_inc(const_ready, 1)
            nc.gpsimd.iota(pos[:], pattern=[[1, S]], base=0, channel_multiplier=0).then_inc(const_ready, 1)
            nc.gpsimd.iota(iota_e[:], pattern=[[0, NT], [1, E]], base=0, channel_multiplier=0).then_inc(const_ready, 1)
            nc.gpsimd.memset(zeros[:], 0.0).then_inc(zero_ready, 1)
            pool.wait_ge(slots_zeroed, 64)
            pool.wait_ge(routed, 1)
            for t in range(NT):
                nc.gpsimd.indirect_dma_start(
                    slots_dram[:, :], bass.IndirectOffsetOnAxis(ap=scatter_to[:, t:t + 1], axis=0), xa[:, t, :], None,
                    bounds_check=E * C - 1, oob_is_err=False).then_inc(scattered, 16)
            pool.wait_ge(scattered, 16 * NT)

        @block.scalar
        def _(act):
            act.wait_ge(var_ready, 1)
            nc.scalar.activation(sd[:, 0, :], moments[:, :, 1], ACT.Sqrt, bias=eps[:, 0:1]).then_inc(sd_ready, 1)
            act.wait_ge(ang_ready, 1)
            nc.scalar.activation(sin[:], ang[:], ACT.Sin).then_inc(sin_ready, 1)
            nc.scalar.activation(cos[:], ang[:], ACT.Sin, scale=0.5).then_inc(sin_ready, 1)
            act.wait_ge(ld_w, 32)
            flat = wraw[:].rearrange("p t m -> p (t m)")
            for q in range(3):
                if q:
                    act.wait_ge(sq_done, q)
                nc.scalar.activation(junk[:], flat[:, q * 2048:(q + 1) * 2048], ACT.Square,
                                     accum_out=wsq[:, q:q + 1]).then_inc(sq_done, 1)
            act.wait_ge(sq_done, 3)
            nc.scalar.activation(junk[:], wo_raw[:].rearrange("p t n -> p (t n)"), ACT.Square,
                                 accum_out=wsq[:, 3:4]).then_inc(sq_done, 1)
            for b in range(NB):
                act.wait_ge(xt_ps, b + 1)
                if b >= 2:
                    act.wait_ge(xt_stored[b % 2], 16 * (b // 2))
                nc.scalar.copy(xth[:, b % 2, 0], psx[b % 2][:]).then_inc(xt_hi, 1)
                if b >= 2:
                    act.wait_ge(logits_ready, b - 1)
                nc.scalar.copy(xt32[:, b % 2], psx[b % 2][:]).then_inc(xt_32, 1)
            act.wait_ge(scale_ready, 1)
            for i in range(NW + NWO):
                act.wait_ge(w_ps, i + 1)
                which = 0 if i < NW else 1
                for o, v in weight_views(wt[0], wot[0], psw[i % 2], i, NW):
                    last = nc.scalar.activation(o, v, ACT.Copy, scale=scale[:, which:which + 1])
                last.then_inc(w_hi, 1)
            act.wait_ge(shifted, 1)
            nc.scalar.activation(rt[:, 2, :], rt[:, 1, :], ACT.Exp).then_inc(exps, 1)

        @block.vector
        def _(dve):
            link = dve_linker(dve, chain)
            nc.vector.memset(eps[:], EPS)
            for b in range(NB):
                dve.wait_ge(ld_x[b], 16)
                for t in range(b * TPB, (b + 1) * TPB):
                    last = nc.vector.bn_stats(stats[:, t, :], xa[:, t, :])
            link(last)
            for t in range(NT):
                last = nc.vector.bn_aggr(moments[:, t, :], stats[:, t, :])
            last.then_inc(var_ready, 1)
            dve.wait_ge(sd_ready, 1)
            link(nc.vector.reciprocal(sd[:, 1, :], sd[:, 0, :]))
            link(nc.vector.scalar_tensor_tensor(out=sd[:, 2, :], in0=moments[:, :, 1], scalar=eps[:, 0:1], in1=sd[:, 1, :], op0=ALU.add, op1=ALU.mult))
            link(nc.vector.tensor_tensor(sd[:, 3, :], sd[:, 0, :], sd[:, 2, :], ALU.add))
            link(nc.vector.tensor_scalar(sd[:, 3, :], sd[:, 3, :], 0.5, None, ALU.mult))
            link(nc.vector.reciprocal(sd[:, 1, :], sd[:, 3, :]))
            for t in range(NT):
                nc.vector.tensor_scalar(xa[:, t, :], xa[:, t, :], moments[:, t, 0:1], sd[:, 1, t:t + 1],
                                        ALU.subtract, ALU.mult).then_inc(xn_ready, 1)
            dve.wait_ge(ld_small, 16 * 7)
            dve.wait_ge(const_ready, 4)
            link(nc.vector.tensor_copy(ang[:], pos[:]))
            link(nc.vector.tensor_scalar(ang[:], ang[:], freq[:, 0:1], None, ALU.mult))
            link(nc.vector.tensor_scalar(turns[:], ang[:], INV_TWO_PI, None, ALU.mult))
            link(nc.vector.tensor_scalar(turns[:], turns[:], ROUND, None, ALU.add))
            link(nc.vector.tensor_scalar(turns[:], turns[:], ROUND, None, ALU.subtract))
            for part in TWO_PI_PARTS:
                link(nc.vector.scalar_tensor_tensor(out=ang[:], in0=turns[:], scalar=-part, in1=ang[:], op0=ALU.mult, op1=ALU.add))
            nc.vector.tensor_scalar(ang[:], ang[:], PI_BELOW, -PI_BELOW, ALU.min, ALU.max).then_inc(ang_ready, 1)
            for b in range(NB):
                dve.wait_ge(xt_hi, b + 1)
                dve.wait_ge(xt_32, b + 1)
                nc.vector.tensor_tensor(xth[:, b % 2, 1], psx[b % 2][:], xth[:, b % 2, 0], ALU.subtract).then_inc(xt_lo, 1)
            dve.wait_ge(sin_ready, 2)
            link(nc.vector.tensor_tensor(cos[:], cos[:], cos[:], ALU.mult))
            link(nc.vector.tensor_scalar(cos[:], cos[:], -2.0, 1.0, ALU.mult, ALU.add))
            dve.wait_ge(n2_ready, 1)
            link(nc.vector.tensor_reduce(n2[:, 0:1], psn[:, 0:3], AX_X, ALU.add))
            link(nc.vector.tensor_copy(n2[:, 1:2], psn[:, 3:4]))
            power_of_two(link, nc, n2[:], expo[:], scale[:], inverse[:])
            nc.vector.tensor_tensor(score_scale[:], inverse[:, 0:1], inverse[:, 0:1], ALU.mult).then_inc(scale_ready, 1)
            dve.wait_ge(scale_ready, 1)
            link(nc.vector.tensor_scalar(score_scale[:], score_scale[:], -float(D) ** -0.5, None, ALU.mult))
            link(nc.vector.tensor_tensor(y_scale[:], inverse[:, 0:1], inverse[:, 1:2], ALU.mult))
            link(nc.vector.tensor_scalar(slope[:], slope[:], 0.01, None, ALU.max))
            link(nc.vector.tensor_scalar(coef[:], raw_p[:], 0.01, None, ALU.max))
            link(nc.vector.tensor_scalar(coef[:], coef[:], -float(D) ** 0.5, None, ALU.mult))
            link(nc.vector.tensor_scalar(coef[:], coef[:], scale[:, 0:1], scale[:, 0:1], ALU.mult, ALU.mult))
            for i in range(NW + NWO):
                dve.wait_ge(w_hi, i + 1)
                which = 0 if i < NW else 1
                for (o, v), (h, _) in zip(weight_views(wt[1], wot[1], psw[i % 2], i, NW), weight_views(wt[0], wot[0], psw[i % 2], i, NW)):
                    last = nc.vector.scalar_tensor_tensor(out=o, in0=v, scalar=scale[:, which:which + 1], in1=h,
                                                          op0=ALU.mult, op1=ALU.subtract)
                last.then_inc(w_lo, 1)
            dve.wait_ge(logits_ready, NB)
            link(nc.vector.tensor_copy(rt[:, 0, :], psg[:]))
            link(nc.vector.tensor_copy(lanes[:], iota_e[:]))
            link(nc.vector.tensor_reduce(col[:, 0, :], logits, AX_X, ALU.max))
            nc.vector.tensor_tensor(r3(1), logits, spread(col[:, 0, :]), ALU.subtract).then_inc(shifted, 1)
            dve.wait_ge(exps, 1)
            link(nc.vector.tensor_reduce(col[:, 1, :], r3(2), AX_X, ALU.add))
            link(nc.vector.reciprocal(col[:, 2, :], col[:, 1, :]))
            link(nc.vector.tensor_scalar(r3(3), r3(1), 0.0, -float(E), ALU.is_ge, ALU.mult))
            link(nc.vector.tensor_tensor(r3(3), r3(3), lanes[:], ALU.add))
            link(nc.vector.tensor_reduce(col[:, 3, :], r3(3), AX_X, ALU.min))
            link(nc.vector.tensor_scalar(col[:, 3, :], col[:, 3, :], float(E), None, ALU.add))
            link(nc.vector.tensor_tensor(r3(4), lanes[:], spread(col[:, 3, :]), ALU.is_equal))
            nc.vector.tensor_copy(onehot[:], rt[:, 4, :]).then_inc(onehot_ready, 1)
            dve.wait_ge(counts_ready, 2)
            link(nc.vector.tensor_copy(rt[:, 1, :], psn[:]))
            link(nc.vector.tensor_copy(rt[:, 5, :], psg[:]))
            src, dst, step = 1, 2, 1
            while step < NT:
                w = step * E
                link(nc.vector.tensor_copy(rt[:, dst, 0:w], rt[:, src, 0:w]))
                link(nc.vector.tensor_tensor(rt[:, dst, w:], rt[:, src, w:], rt[:, src, 0:NT * E - w], ALU.add))
                src, dst = dst, (3 if dst == 2 else 2)
                step *= 2
            link(nc.vector.tensor_tensor(rt[:, src, :], rt[:, src, :], rt[:, 1, :], ALU.subtract))
            link(nc.vector.tensor_tensor(rt[:, src, :], rt[:, src, :], rt[:, 5, :], ALU.add))
            link(nc.vector.tensor_tensor(rt[:, src, :], rt[:, src, :], rt[:, 4, :], ALU.mult))
            link(nc.vector.tensor_reduce(col[:, 4, :], r3(src), AX_X, ALU.add))
            link(nc.vector.tensor_scalar(col[:, 5, :], col[:, 3, :], float(C), None, ALU.mult))
            link(nc.vector.tensor_scalar(col[:, 6, :], col[:, 4, :], float(C), None, ALU.is_ge))
            link(nc.vector.scalar_tensor_tensor(out=col[:, 7, :], in0=col[:, 6, :], scalar=float(2 * E * C), in1=col[:, 4, :], op0=ALU.mult, op1=ALU.add))
            link(nc.vector.tensor_tensor(scatter_to[:], col[:, 7, :], col[:, 5, :], ALU.add))
            link(nc.vector.scalar_tensor_tensor(out=gather_from[:], in0=col[:, 4, :], scalar=float(C - 1), in1=col[:, 5, :], op0=ALU.min, op1=ALU.add))
            link(nc.vector.tensor_scalar(col[:, 6, :], col[:, 6, :], -1.0, 1.0, ALU.mult, ALU.add))
            nc.vector.tensor_tensor(gate[:], col[:, 6, :], col[:, 2, :], ALU.mult).then_inc(routed, 1)

        @block.tensor
        def _(pe):
            def logits_of(b):
                pe.wait_ge(xt_32, b + 1)
                for t in range(TPB):
                    n = b * TPB + t
                    for k in range(KT):
                        last = nc.tensor.matmul(psg[:, n * E:(n + 1) * E], xt32[:, b % 2, k, t * P:(t + 1) * P],
                                                wg_sb[:, k, :], start=(k == 0), stop=(k == KT - 1))
                last.then_inc(logits_ready, 1)

            pe.wait_ge(const_ready, 1)
            pe.wait_ge(ld_small, 16 * 7)
            for b in range(NB):
                if b >= 2:
                    pe.wait_ge(xt_lo, b - 1)
                pe.wait_ge(xn_ready, (b + 1) * TPB)
                for k in range(KT):
                    for t in range(TPB):
                        last = nc.tensor.transpose(psx[b % 2][:, k, t * P:(t + 1) * P],
                                                   xa[:, b * TPB + t, k * P:(k + 1) * P], ident[:])
                last.then_inc(xt_ps, 1)
                if b:
                    logits_of(b - 1)
            logits_of(NB - 1)
            pe.wait_ge(sq_done, 4)
            nc.tensor.matmul(psn[:, 0:4], ones[:], wsq[:], start=True, stop=True).then_inc(n2_ready, 1)
            pe.wait_ge(ld_w, 32)
            for i in range(NW + NWO):
                if i >= 2:
                    pe.wait_ge(w_lo, i - 1)
                for q in range(4):
                    if i < NW:
                        k, t = i // (NW // KT), 4 * (i % (NW // KT)) + q
                        src = wraw[:, t, k * P:(k + 1) * P]
                    else:
                        k, t = 2 * (i - NW) + q // 2, q % 2
                        src = wo_raw[:, t, k * P:(k + 1) * P]
                    last = nc.tensor.transpose(psw[i % 2][:, q * P:(q + 1) * P], src, ident[:])
                last.then_inc(w_ps, 1)
            pe.wait_ge(onehot_ready, 1)
            pe.wait_ge(const_ready, 2)
            nc.tensor.matmul(psg[:], before[:], onehot[:], start=True, stop=True).then_inc(counts_ready, 1)
            nc.tensor.matmul(psn[:], onesh[:], onehot[:], start=True, stop=True).then_inc(counts_ready, 1)


def weight_views(w, wo, bank, i, nw):
    if i >= nw:
        k = 2 * (i - nw)
        return [(wo[:, k:k + 2, :], bank[:].rearrange("p (k n) -> p k n", k=2))]
    per = nw // KT
    k, c = i // per, i % per * BANK
    if c >= 2 * H * D:
        return [(w[:, k, c:c + BANK], bank[:])]
    found = []
    for g in range(2):
        a = c + g * HG * D
        for f in range(2):
            found.append((w[:, k, a + f * P:a + (f + 1) * P].rearrange("p (h j) -> p h j", h=HG),
                          bank[:, g * HG * D:(g + 1) * HG * D].rearrange("p (h f j) -> p h f j", h=HG, f=2)[:, :, f, :]))
    return found


def experts(nc, sem, x_tiles, w1, w2, slots_dram, expert_dram, base_dram, ident, gather_from, gate):
    FT = F // P
    CT = C // P
    with ExitStack() as ctx:
        def sb(name, shape, dt=F32):
            return ctx.enter_context(nc.sbuf_tensor(name, shape, dt))

        raw = sb("raw", [P, 2, 2, 2048])
        whi = sb("whi", [P, 2, 2, 2048], F16)
        wlo = sb("wlo", [P, 2, 2, 2048], F16)
        rows = sb("rows", [P, 2, CT, M])
        dt = sb("dt", [P, 2, 2, KT, C], F16)
        hid = sb("hid", [P, 2, 2, FT, C], F16)
        eo = sb("eo", [P, 2, CT, M])
        junk = sb("junk_e", [P, 2048])
        wsq = sb("wsq_e", [P, 2, 2])
        n2 = sb("n2_e", [P, 2])
        expo = sb("expo_e", [P, 2], I32)
        scale = sb("scale_e", [P, 2, 2])
        inverse = sb("inverse_e", [P, 2])
        un = sb("un_e", [P, 2, 1])
        onesf = sb("ones_e", [P, P])
        got = sb("got", [P, 4, M])
        xres = sb("xres", [P, 2, TPB, M])
        psd = ctx.enter_context(nc.psum_tensor("psd", [P, KT, C], F32))
        psh = [ctx.enter_context(nc.psum_tensor(f"psh{i}", [P, BANK], F32)) for i in range(2)]
        pso = ctx.enter_context(nc.psum_tensor("pso", [P, CT, M], F32))
        psn = ctx.enter_context(nc.psum_tensor("psn_e", [P, BANK], F32))

        ld_w = [sem(f"ld_we{r}") for r in range(2)]
        ld_rows = [sem(f"ld_rows{r}") for r in range(2)]
        ones_ready = sem("ones_e_ready")
        chain, sq_done, n2_ready = sem("chain_b"), sem("sq_e"), sem("n2_e_ready")
        scale_ready, w_split = sem("scale_e_ready"), sem("w_split")
        d_ps, d_hi, d_lo = sem("d_ps"), sem("d_hi"), sem("d_lo")
        h_ps, h_hi, h_lo = sem("h_ps"), sem("h_hi"), sem("h_lo")
        o_ps, o_sb, combined = sem("o_ps"), sem("o_sb"), sem("combined")
        o_stored = [sem(f"o_stored{r}") for r in range(2)]
        ld_xres = [sem(f"ld_xres{r}") for r in range(2)]
        base_stored = [sem(f"base_stored{r}") for r in range(2)]
        gathered = [sem(f"gathered{r}") for r in range(4)]
        block = ctx.enter_context(nc.Block())
        w1v = w1.rearrange("e (k p) f -> e p k f", p=P)
        w2v = w2.rearrange("e (t p) m -> e p t m", p=P)
        rows_v = slots_dram.rearrange("(e t p) m -> e p t m", p=P, t=CT)
        eo_v = expert_dram.rearrange("(e t p) m -> e p t m", p=P, t=CT)

        went_on = sem("went_on_e")

        def over_experts(eng, one):
            one(0, 0)
            one(0, 1)
            with eng.Fori(1, E // 2) as n:
                one(n, 0)
                one(n, 1)

        def later(e):
            return not isinstance(e, int)

        @block.sync
        def _(sp):
            def load(n, r):
                e = 2 * n + r
                if later(e):
                    split, turned = sp.snap(2 * e - 2), sp.snap(e - 1)
                    sp.wait_ge(w_split, split)
                    sp.sem_inc(went_on)
                    sp.wait_ge(d_ps, turned)
                    sp.sem_inc(went_on)
                sp.dma_start(raw[:, r, 0, :].rearrange("p (k f) -> p k f", k=KT), w1v[e]).then_inc(ld_w[r], 16)
                sp.dma_start(raw[:, r, 1, :].rearrange("p (t m) -> p t m", t=FT), w2v[e]).then_inc(ld_w[r], 16)
                sp.dma_start(rows[:, r], rows_v[e]).then_inc(ld_rows[r], 16)

            over_experts(sp, load)
            for b in range(NB):
                if b >= 2:
                    sp.wait_ge(base_stored[b % 2], 16 * (b // 2))
                sp.dma_start(xres[:, b % 2], x_tiles[:, b * TPB:(b + 1) * TPB, :]).then_inc(ld_xres[b % 2], 16)
                if b:
                    sp.wait_ge(combined, TPB * b)
                    sp.dma_start(base_dram[b - 1], xres[:, (b - 1) % 2].rearrange("p t m -> p (t m)")).then_inc(base_stored[(b - 1) % 2], 16)
            sp.wait_ge(combined, TPB * NB)
            sp.dma_start(base_dram[NB - 1], xres[:, (NB - 1) % 2].rearrange("p t m -> p (t m)")).then_inc(base_stored[1], 16)
            for r in range(2):
                sp.wait_ge(base_stored[r], 16 * (NB // 2))

        @block.gpsimd
        def _(pool):
            nc.gpsimd.memset(onesf[:], 1.0).then_inc(ones_ready, 1)

            def store(n, r):
                e = 2 * n + r
                pool.wait_ge(o_sb, e + 1)
                pool.dma_start(eo_v[e], eo[:, r]).then_inc(o_stored[r], 16)

            over_experts(pool, store)
            for r in range(2):
                pool.wait_ge(o_stored[r], 16 * (E // 2))
            for t in range(NT):
                if t >= 4:
                    pool.wait_ge(combined, t - 3)
                nc.gpsimd.indirect_dma_start(
                    got[:, t % 4, :], None, expert_dram[:, :], bass.IndirectOffsetOnAxis(ap=gather_from[:, t:t + 1], axis=0),
                    bounds_check=E * C - 1, oob_is_err=False).then_inc(gathered[t % 4], 16)
            for q in range(4):
                pool.wait_ge(gathered[q], 16 * (NT // 4))

        @block.scalar
        def _(act):
            def squares(n, r):
                e = 2 * n + r
                act.wait_ge(ld_w[r], 32 * n + 32)
                for w in range(2):
                    if later(e) or e + w:
                        act.wait_ge(sq_done, 2 * e + w)
                    if w == 0 and later(e):
                        act.wait_ge(n2_ready, e - 1)
                    nc.scalar.activation(junk[:], raw[:, r, w, :], ACT.Square, accum_out=wsq[:, r, w:w + 1]).then_inc(sq_done, 1)

            def one(n, r):
                e = 2 * n + r
                squares(n, r)
                act.wait_ge(d_ps, e + 1)
                if later(e):
                    act.wait_ge(h_ps, 4 * e - 4)
                nc.scalar.copy(dt[:, r, 0], psd[:]).then_inc(d_hi, 1)
                for q in range(4):
                    act.wait_ge(h_ps, 4 * e + q + 1)
                    if q == 0 and later(e):
                        act.wait_ge(o_ps, e - 1)
                    nc.scalar.activation(hid[:, r, 0, 2 * q:2 * q + 2, :], psh[q % 2][:].rearrange("p (f c) -> p f c", f=2), ACT.Relu).then_inc(h_hi, 1)
                act.wait_ge(o_ps, e + 1)
                if later(e):
                    act.wait_ge(o_stored[r], 16 * n)
                nc.scalar.activation(eo[:, r], pso[:], ACT.Copy, scale=un[:, r, 0:1]).then_inc(o_sb, 1)

            over_experts(act, one)

        @block.vector
        def _(dve):
            def one(n, r):
                e = 2 * n + r
                dve.wait_ge(n2_ready, e + 1)
                c = [0]

                def link(ins):
                    c[0] += 1
                    ins.then_inc(chain, 1)
                    dve.wait_ge(chain, e * 12 + c[0])

                link(nc.vector.tensor_copy(n2[:], psn[:, 0:2]))
                power_of_two(link, nc, n2[:], expo[:], scale[:, r, :], inverse[:])
                if later(e):
                    dve.wait_ge(o_sb, e - 1)
                link(nc.vector.tensor_tensor(un[:, r, :], inverse[:, 0:1], inverse[:, 1:2], ALU.mult))
                if later(e):
                    dve.wait_ge(o_ps, e - 1)
                for w in range(2):
                    link(nc.vector.tensor_scalar(whi[:, r, w, :], raw[:, r, w, :], scale[:, r, w:w + 1], None, ALU.mult))
                    nc.vector.scalar_tensor_tensor(out=wlo[:, r, w, :], in0=raw[:, r, w, :], scalar=scale[:, r, w:w + 1],
                                                   in1=whi[:, r, w, :], op0=ALU.mult, op1=ALU.subtract).then_inc(w_split, 1)
                dve.wait_ge(d_hi, e + 1)
                nc.vector.tensor_tensor(dt[:, r, 1], psd[:], dt[:, r, 0], ALU.subtract).then_inc(d_lo, 1)
                for q in range(4):
                    dve.wait_ge(h_hi, 4 * e + q + 1)
                    nc.vector.scalar_tensor_tensor(out=hid[:, r, 1, 2 * q:2 * q + 2, :], in0=psh[q % 2][:].rearrange("p (f c) -> p f c", f=2), scalar=0.0,
                                                   in1=hid[:, r, 0, 2 * q:2 * q + 2, :], op0=ALU.max, op1=ALU.subtract).then_inc(h_lo, 1)

            over_experts(dve, one)
            for t in range(NT):
                dve.wait_ge(gathered[t % 4], 16 * (t // 4 + 1))
                dve.wait_ge(ld_xres[t // TPB % 2], 16 * (t // TPB // 2 + 1))
                xt = xres[:, t // TPB % 2, t % TPB, :]
                nc.vector.scalar_tensor_tensor(out=xt, in0=got[:, t % 4, :], scalar=gate[:, t:t + 1], in1=xt,
                                               op0=ALU.mult, op1=ALU.add).then_inc(combined, 1)

        @block.tensor
        def _(pe):
            PARTS = ((0, 0), (0, 1), (1, 0))
            split = (whi, wlo)
            pe.wait_ge(ones_ready, 1)

            def one(n, r):
                e = 2 * n + r
                pe.wait_ge(sq_done, 2 * e + 2)
                if later(e) or e:
                    pe.wait_ge(d_lo, e)
                nc.tensor.matmul(psn[:, 0:2], onesf[:], wsq[:, r, :], start=True, stop=True).then_inc(n2_ready, 1)
                pe.wait_ge(ld_rows[r], 16 * n + 16)
                for k in range(KT):
                    for t in range(CT):
                        last = nc.tensor.transpose(psd[:, k, t * P:(t + 1) * P], rows[:, r, t, k * P:(k + 1) * P], ident[:])
                last.then_inc(d_ps, 1)
                pe.wait_ge(w_split, 2 * e + 2)
                pe.wait_ge(d_lo, e + 1)
                for q in range(4):
                    if later(e) or e or q >= 2:
                        pe.wait_ge(h_lo, 4 * e + q - 1)
                    for f in range(2):
                        m = 0
                        for k in range(KT):
                            for a, b in PARTS:
                                fc = k * F + (2 * q + f) * P
                                last = nc.tensor.matmul(psh[q % 2][:, f * C:(f + 1) * C], split[a][:, r, 0, fc:fc + P],
                                                        dt[:, r, b, k, :], start=(m == 0), stop=(m == 3 * KT - 1))
                                m += 1
                    last.then_inc(h_ps, 1)
                pe.wait_ge(h_lo, 4 * e + 4)
                if later(e) or e:
                    pe.wait_ge(o_sb, e)
                for t in range(CT):
                    m = 0
                    for f in range(FT):
                        for a, b in PARTS:
                            last = nc.tensor.matmul(pso[:, t, :], hid[:, r, a, f, t * P:(t + 1) * P],
                                                    split[b][:, r, 1, f * M:(f + 1) * M], start=(m == 0), stop=(m == 3 * FT - 1))
                            m += 1
                last.then_inc(o_ps, 1)

            over_experts(pe, one)


def attention(nc, sem, out, xt_dram, base_dram, ident, wt, wot, cos, sin, score_scale, y_scale, coef, slope):
    with ExitStack() as ctx:
        def sb(name, shape, dt=F32):
            return ctx.enter_context(nc.sbuf_tensor(name, shape, dt))

        strips = sb("strips", [P, H, SW])
        xcur = sb("xcur", [P, 2, KT, S], F16)
        proj = sb("proj", [P, 2, 2, S])
        prod = sb("prod", [P, 4, S])
        rot = sb("rot", [P, 2, 2, S])
        parts = sb("parts", [P, 2, 2, 2, S], F16)
        qk = sb("qk", [P, 2, 2, HG, S], F16)
        kswap = sb("kswap", [P, 2, HG, S], F16)
        val = [sb(f"val_{n}", [P, 4, TPB, HG * D], F16) for n in ("hi", "lo")]
        neg = sb("neg", [P, 2, 2, S])
        neg_max = sb("neg_max", [P, 4])
        prob = sb("prob", [P, 2, 2, S])
        sums = sb("sums", [P, 2, 8])
        rsum = sb("rsum", [P, 8])
        pt = [sb(f"pt_{n}", [P, 2, 2, TPB, P], F16) for n in ("hi", "lo")]
        ctxt = sb("ctxt", [P, TPB, HG * D])
        ot = [sb(f"ot_{n}", [P, 2, S], F16) for n in ("hi", "lo")]
        yacc = sb("yacc", [P, TPB, M])

        ps_s = [ctx.enter_context(nc.psum_tensor(f"ps_s{i}", [P, BANK], F32)) for i in range(2)]
        ps_t = [ctx.enter_context(nc.psum_tensor(f"ps_t{i}", [P, 2, BANK], F32)) for i in range(2)]
        ps_o = ctx.enter_context(nc.psum_tensor("ps_o", [P, BANK], F32))
        ps_x = ctx.enter_context(nc.psum_tensor("ps_x", [P, BANK], F32))

        dist_ready, ln_ready, strips_ready = sem("dist_ready"), sem("ln_ready"), sem("strips_ready")
        chain, chain_d = sem("chain_c"), sem("distances")
        x_loaded, base_loaded, y_stored = sem("x_loaded"), sem("base_loaded"), sem("y_stored")
        qk_moved = [sem(f"qk_moved{r}") for r in range(2)]
        scored = sem("scored")
        negated = sem("negated")
        exp_done = sem("exp_done")
        turned, turned_hi, turned_lo = sem("turned"), sem("turned_hi"), sem("turned_lo")
        pv_done = sem("pv_done")
        ctx_read = sem("ctx_read")
        filled, x_free = sem("filled"), sem("x_free")
        val_hi = sem("val_hi")
        turned_parts = sem("rotations")
        parts_hi, parts_lo = sem("parts_hi"), sem("parts_lo")

        went_on = sem("went_on")

        def fills_before(b, l):
            n = 2 * FILLS + PAIRS * b + l
            n = n - (min(max(l - 6, 0), 2) if isinstance(b, int) and b == 0 else 2)
            if isinstance(b, int) and b == NB - 1:
                n -= sum(m // 8 >= 2 and m % 8 < FILLS for m in range(l))
            return n

        def pair_item(l):
            return 9 * (l // 8) + l % 8 + (l % 8 > 3)

        def items(b, n):
            if isinstance(b, int) and b == 0:
                return n + 1 - (n >= 0) - (n >= 4)
            return 36 * b + n + 1 - 2

        def wait(eng, s, v):
            if not isinstance(v, int) or v > 0:
                eng.wait_ge(s, v)

        def over_batches(eng, batch):
            batch(0)
            with eng.Fori(1, NB - 1) as b:
                batch(b)
            batch(NB - 1)

        def is_first(b):
            return isinstance(b, int) and b == 0

        def is_last(b):
            return isinstance(b, int) and b == NB - 1

        def ahead(b, j):
            if is_last(b) and j >= 2:
                return None
            return 2 * b + j // 2 + 1, j % 2, (j + 2) % 4

        def slot_kind(b, l):
            j, k = divmod(l, 8)
            if k < FILLS:
                return ahead(b, j) and ("qk" if k < 4 else "v", k if k < 4 else k - 4, *ahead(b, j))
            return None if is_first(b) and j == 0 else ("y", k - FILLS)

        def wait_parts_moved(eng, n, r):
            if r:
                eng.wait_ge(qk_moved[0], 512 * (n + 1))
            else:
                wait(eng, qk_moved[1], 512 * n)

        block = ctx.enter_context(nc.Block())

        @block.sync
        def _(sp):
            def move(n, r):
                F = 2 * n + r
                wait(sp, scored, 16 * (F - 1))
                sp.wait_ge(parts_lo, 2 * F + 2)
                for h in range(HG):
                    rows = slice(32 * h, 32 * h + 32)
                    for q in range(4):
                        a, c = 32 * q, 32 * ((q + 2) % 4)
                        sp.dma_start(qk[a:a + 32, r, :, h, :], parts[rows, q // 2, :, q % 2, :]).then_inc(qk_moved[r], 16)
                        sp.dma_start(kswap[c:c + 32, r, h, :], parts[rows, q // 2, 1, q % 2, :]).then_inc(qk_moved[r], 16)

            def load_x(b):
                sp.dma_start(xcur[:].rearrange("p h k s -> p (h k s)"), xt_dram[b]).then_inc(x_loaded, 16)

            def batch(b):
                for j in range(4):
                    if j == 1 and not is_last(b):
                        sp.wait_ge(filled, fills_before(b, 14))
                        sp.sem_inc(went_on)
                        load_x(b + 1)
                    if ahead(b, j):
                        move(*ahead(b, j)[:2])

            load_x(0)
            move(0, 0)
            move(0, 1)
            over_batches(sp, batch)
            sp.wait_ge(x_free, fills_before(NB - 1, PAIRS) + 2)
            sp.dma_start(out[NB - 1].rearrange("(t p) m -> p t m", p=P), yacc[:]).then_inc(y_stored, 16)
            sp.wait_ge(y_stored, 16 * NB)

        @block.gpsimd
        def _(pool):
            nc.gpsimd.iota(strips[:, 0, :].bitcast(I32), pattern=[[1, SW]], base=-(SW - S),
                           channel_multiplier=-1).then_inc(dist_ready, 1)

            def turn(F, w, n):
                done = 6 * (2 * F + w)
                pool.wait_ge(x_free, n)
                wait(pool, turned_parts, done)
                for i, (half, table) in enumerate(((0, cos), (1, sin), (0, sin), (1, cos))):
                    nc.gpsimd.tensor_tensor(prod[:, i, :], proj[:, w, half, :], table[:], ALU.mult).then_inc(turned_parts, 1)
                pool.wait_ge(turned_parts, done + 4)
                wait(pool, parts_lo, 2 * F - 1 + w)
                nc.gpsimd.tensor_tensor(rot[:, w, 0, :], prod[:, 0, :], prod[:, 1, :], ALU.subtract).then_inc(turned_parts, 1)
                nc.gpsimd.tensor_tensor(rot[:, w, 1, :], prod[:, 2, :], prod[:, 3, :], ALU.add).then_inc(turned_parts, 1)

            def step(F, fills):
                turn(F, 0, fills + 2)
                turn(F, 1, fills + 4)
                for w in range(2):
                    pool.wait_ge(parts_hi, 2 * F + w + 1)
                    nc.gpsimd.tensor_tensor(parts[:, 1, w], rot[:, w], parts[:, 0, w], ALU.subtract).then_inc(parts_lo, 1)

            def batch(b):
                for j in range(4):
                    if ahead(b, j):
                        n, r, _ = ahead(b, j)
                        step(2 * n + r, fills_before(b, 8 * j))

            step(0, 0)
            step(1, FILLS)
            over_batches(pool, batch)

        @block.scalar
        def _(act):
            act.wait_ge(dist_ready, 2)
            for i in range(H):
                h = (i + 1) % H
                nc.scalar.activation(strips[:, h, :], strips[:, 0, :], ACT.Ln, bias=1.0,
                                     scale=slope[:, h:h + 1]).then_inc(ln_ready, 1)

            def read_fill(kind, fill):
                what, k = kind[:2]
                if what == "y":
                    return
                n, r, _ = kind[2:]
                F = 2 * n + r
                act.wait_ge(filled, fill + 1)
                if what == "qk":
                    wait(act, turned_parts, 6 * (2 * F - 2 + k // 2) + 4)
                    nc.scalar.copy(proj[:, k // 2, k % 2, :], ps_x[:]).then_inc(x_free, 1)
                else:
                    nc.scalar.copy(val[0][:, kind[4], 2 * k:2 * k + 2, :],
                                   ps_x[:].rearrange("p (t n) -> p t n", t=2)).then_inc(val_hi, 1)

            def high(n, r, w):
                act.wait_ge(turned_parts, 6 * (4 * n + 2 * r + w) + 6)
                wait_parts_moved(act, n, r)
                nc.scalar.copy(parts[:, 0, w], rot[:, w]).then_inc(parts_hi, 1)

            def pair_hi(b, l):
                item = pair_item(l)
                act.wait_ge(turned, items(b, item))
                wait(act, pv_done, PAIRS * b + l - 2)
                nc.scalar.activation(pt[0][:, (l - 1) % 2].rearrange("p q k c -> p q (k c)"), ps_t[item % 2][:],
                                     ACT.Copy, scale=P_SCALE).then_inc(turned_hi, 1)

            def ctx_hi(b, item):
                act.wait_ge(turned, items(b, item))
                nc.scalar.activation(ot[0][:], ps_t[item % 2][:], ACT.Copy, scale=1.0 / P_SCALE).then_inc(turned_hi, 1)

            def slot(b, l):
                s = PAIRS * b + l
                j, k = divmod(l, 8)
                for q in range(2):
                    act.wait_ge(negated, 2 * s + q + 1)
                    if q == 0:
                        wait(act, turned, items(b, pair_item(l - 1)))
                    nc.scalar.activation(prob[:, l % 2, q, :], neg[:, l % 2, q, :], ACT.Exp,
                                         bias=neg_max[:, 2 * (l % 2) + q:2 * (l % 2) + q + 1], scale=-1.0,
                                         accum_out=sums[:, l // 4 % 2, 2 * (l % 4) + q:2 * (l % 4) + q + 1]).then_inc(exp_done, 1)
                kind = slot_kind(b, l)
                if kind:
                    read_fill(kind, fills_before(b, l))
                if l or not is_first(b):
                    pair_hi(b, l)
                if k == 3 and not (is_first(b) and j == 0):
                    ctx_hi(b, 9 * j + 4)
                if k in (5, 7) and ahead(b, j):
                    high(*ahead(b, j)[:2], k // 7)
                if l == 9 and not is_first(b):
                    act.wait_ge(x_free, fills_before(b, 8))
                    act.dma_start(out[b - 1].rearrange("(t p) m -> p t m", p=P), yacc[:]).then_inc(y_stored, 16)
                if l == 11:
                    wait(act, y_stored, 16 * b)
                    act.dma_start(yacc[:].rearrange("p t m -> p (t m)"), base_dram[b]).then_inc(base_loaded, 16)

            for F in range(2):
                for k in range(FILLS):
                    read_fill(("qk" if k < 4 else "v", k if k < 4 else k - 4, 0, F, F), FILLS * F + k)
                high(0, F, 0)
                high(0, F, 1)

            def batch(b):
                for l in range(PAIRS):
                    slot(b, l)

            over_batches(act, batch)
            pair_hi(NB - 1, PAIRS)
            ctx_hi(NB - 1, 37)

        @block.vector
        def _(dve):
            dve.wait_ge(dist_ready, 1)
            nc.vector.tensor_copy(strips[:, 1, :], strips[:, 0, :].bitcast(I32)).then_inc(chain_d, 1)
            dve.wait_ge(chain_d, 1)
            nc.vector.scalar_tensor_tensor(out=strips[:, 0, :], in0=strips[:, 1, :], scalar=-1.0, in1=strips[:, 1, :],
                                           op0=ALU.mult, op1=ALU.max).then_inc(dist_ready, 1)
            for i in range(H):
                h = (i + 1) % H
                dve.wait_ge(ln_ready, H if h == 0 else i + 1)
                nc.vector.tensor_scalar(strips[:, h, :], strips[:, h, :], coef[:, h:h + 1], None, ALU.mult).then_inc(strips_ready, 1)
            dve.wait_ge(strips_ready, H)

            def read_fill(kind, b, l, fill):
                what, k = kind[:2]
                if what == "v":
                    n, r, _ = kind[2:5]
                    dve.wait_ge(val_hi, 4 * n + 2 * r + k + 1)
                    nc.vector.tensor_tensor(val[1][:, kind[4], 2 * k:2 * k + 2, :], ps_x[:].rearrange("p (t n) -> p t n", t=2),
                                            val[0][:, kind[4], 2 * k:2 * k + 2, :], ALU.subtract).then_inc(x_free, 1)
                elif what == "y":
                    dve.wait_ge(filled, fill + 1)
                    if l // 8 == 1:
                        dve.wait_ge(base_loaded, 16 * b + 16)
                    part = yacc[:, 2 * k:2 * k + 2, :].rearrange("p t m -> p (t m)")
                    nc.vector.scalar_tensor_tensor(out=part, in0=ps_x[:], scalar=y_scale[:, 0:1], in1=part,
                                                   op0=ALU.mult, op1=ALU.add).then_inc(x_free, 1)

            def pair_lo(b, l):
                item = pair_item(l)
                dve.wait_ge(turned_hi, items(b, item))
                nc.vector.scalar_tensor_tensor(out=pt[1][:, (l - 1) % 2].rearrange("p q k c -> p q (k c)"), in0=ps_t[item % 2][:],
                                               scalar=P_SCALE, in1=pt[0][:, (l - 1) % 2].rearrange("p q k c -> p q (k c)"),
                                               op0=ALU.mult, op1=ALU.subtract).then_inc(turned_lo, 1)

            def ctx_lo(b, item):
                dve.wait_ge(turned_hi, items(b, item))
                nc.vector.scalar_tensor_tensor(out=ot[1][:], in0=ps_t[item % 2][:], scalar=1.0 / P_SCALE, in1=ot[0][:],
                                               op0=ALU.mult, op1=ALU.subtract).then_inc(turned_lo, 1)

            def read_context(b, l):
                unit = PAIRS // 4 * b + (l - 6) // 4
                two = (l - 6) // 4 % 2
                dve.wait_ge(pv_done, PAIRS * b + l - 2)
                if not two:
                    wait(dve, turned, items(b, 9 * (l // 8) + 4))
                nc.vector.reciprocal(rsum[:], sums[:, two, :]).then_inc(chain, 1)
                dve.wait_ge(chain, unit + 1)
                nc.vector.tensor_tensor(ctxt[:, :, two * P:two * P + P].rearrange("p t (h d) -> p h t d", h=2),
                                        ps_o[:].rearrange("p (h t d) -> p h t d", h=2, t=TPB),
                                        rsum[:].rearrange("p (h t) -> p h t", h=2).unsqueeze(3).to_broadcast([P, 2, TPB, D]),
                                        ALU.mult).then_inc(ctx_read, 1)

            def slot(b, l):
                s = PAIRS * b + l
                j, k = divmod(l, 8)
                h = HG * j + k // 2
                for q in range(2):
                    start = SW - S - (2 * (l % 2) + q) * P
                    dve.wait_ge(scored, 2 * s + q + 1)
                    wait(dve, exp_done, 2 * s - 3 + q)
                    dve.sem_inc(went_on)
                    i = 2 * (l % 2) + q
                    nc.vector.tensor_tensor_reduce(neg[:, l % 2, q, :], ps_s[q][:], strips[:, h, start:start + S],
                                                   score_scale[:, 0:1], 3.0e38, ALU.add, ALU.min,
                                                   neg_max[:, i:i + 1]).then_inc(negated, 1)
                if l % 4 == 2 and not (is_first(b) and l == 2):
                    read_context(b, l)
                kind = slot_kind(b, l)
                if kind:
                    read_fill(kind, b, l, fills_before(b, l))
                if l or not is_first(b):
                    pair_lo(b, l)
                if k == 3 and not (is_first(b) and j == 0):
                    ctx_lo(b, 9 * j + 4)

            for F in range(2):
                for k in range(2):
                    read_fill(("v", k, 0, F, F), 0, 0, 0)

            def batch(b):
                for l in range(PAIRS):
                    slot(b, l)

            over_batches(dve, batch)
            pair_lo(NB - 1, PAIRS)
            read_context(NB - 1, PAIRS + 2)
            ctx_lo(NB - 1, 37)
            for k in range(2):
                read_fill(("y", k), NB - 1, 0, fills_before(NB - 1, PAIRS) + k)

        @block.tensor
        def _(pe):
            PARTS = ((0, 0), (0, 1), (1, 0))

            def fill(kind, b, l, fill):
                what, k = kind[:2]
                wait(pe, x_free, fill)
                if what == "qk":
                    g = kind[4]
                    c = k // 2 * H * D + g * HG * D + k % 2 * P
                    m = 0
                    for kt in range(KT):
                        for a, x in PARTS:
                            last = nc.tensor.matmul(ps_x[:], wt[a][:, kt, c:c + P], xcur[:, x, kt, :],
                                                    start=(m == 0), stop=(m == 3 * KT - 1))
                            m += 1
                elif what == "v":
                    c = 2 * H * D + kind[4] * HG * D
                    for i in range(2):
                        t = (2 * k + i) * P
                        m = 0
                        for kt in range(KT):
                            for x, a in PARTS:
                                last = nc.tensor.matmul(ps_x[:, i * M:(i + 1) * M], xcur[:, x, kt, t:t + P],
                                                        wt[a][:, kt, c:c + HG * D], start=(m == 0), stop=(m == 3 * KT - 1))
                                m += 1
                else:
                    g = (l // 8 - 1) % 4
                    for i in range(2):
                        t = (2 * k + i) * P
                        m = 0
                        for kt in range(2):
                            for x, a in PARTS:
                                last = nc.tensor.matmul(ps_x[:, i * M:(i + 1) * M], ot[x][:, kt, t:t + P],
                                                        wot[a][:, 2 * g + kt, :], start=(m == 0), stop=(m == 5))
                                m += 1
                last.then_inc(filled, 1)

            def scores(b, l):
                s = PAIRS * b + l
                j, k = divmod(l, 8)
                if k == 0:
                    pe.wait_ge(qk_moved[j % 2], 512 * (2 * b + j // 2 + 1))
                for q in range(2):
                    t = (2 * (l % 2) + q) * P
                    wait(pe, negated, 2 * s - 1 + q)
                    nc.tensor.matmul(ps_s[q][:], qk[:, j % 2, 0, k // 2, t:t + P], qk[:, j % 2, 1, k // 2, :], start=True, stop=False)
                    nc.tensor.matmul(ps_s[q][:], qk[:, j % 2, 0, k // 2, t:t + P], kswap[:, j % 2, k // 2, :],
                                     start=False, stop=True).then_inc(scored, 1)

            def transposes(b, l):
                s = PAIRS * b + l
                item = pair_item(l)
                wait(pe, turned_lo, items(b, item - 2))
                for q in range(2):
                    pe.wait_ge(exp_done, 2 * s - 1 + q)
                    for kt in range(TPB):
                        last = nc.tensor.transpose(ps_t[item % 2][:, q, kt * P:(kt + 1) * P],
                                                   prob[:, (l - 1) % 2, q, kt * P:(kt + 1) * P], ident[:])
                last.then_inc(turned, 1)

            def context_transposes(b, item, units):
                wait(pe, turned_lo, items(b, item - 2))
                pe.wait_ge(ctx_read, units)
                for kt in range(2):
                    for t in range(TPB):
                        last = nc.tensor.transpose(ps_t[item % 2][:, kt, t * P:(t + 1) * P],
                                                   ctxt[:, t, kt * P:(kt + 1) * P], ident[:])
                last.then_inc(turned, 1)

            def values(b, l):
                l2 = l - 2
                hd = l2 % 8 // 2 * D
                if l2 % 4 == 0:
                    wait(pe, ctx_read, PAIRS // 4 * b + l2 // 4)
                pe.wait_ge(turned_lo, items(b, pair_item(l - 1)))
                for q in range(2):
                    c = (l2 % 4 // 2 * TPB + 2 * (l2 % 2) + q) * D
                    m = 0
                    for kt in range(TPB):
                        for x, a in PARTS:
                            last = nc.tensor.matmul(ps_o[:, c:c + D], pt[x][:, l % 2, q, kt, :],
                                                    val[a][:, l2 // 8 % 4, kt, hd:hd + D], start=(m == 0), stop=(m == 3 * TPB - 1))
                            m += 1
                last.then_inc(pv_done, 1)

            def slot(b, l):
                j, k = divmod(l, 8)
                scores(b, l)
                kind = slot_kind(b, l)
                if kind:
                    if l == 16 and not is_last(b):
                        pe.wait_ge(x_loaded, 16 * b + 32)
                    if kind[0] == "y" and k == FILLS:
                        pe.wait_ge(turned_lo, items(b, 9 * j + 4))
                    fill(kind, b, l, fills_before(b, l))
                if l or not is_first(b):
                    transposes(b, l)
                if k == 3 and not (is_first(b) and j == 0):
                    context_transposes(b, 9 * j + 4, PAIRS // 4 * b + 2 * j)
                if l >= 2 or not is_first(b):
                    values(b, l)

            pe.wait_ge(x_loaded, 16)
            for F in range(2):
                for k in range(FILLS):
                    fill(("qk" if k < 4 else "v", k if k < 4 else k - 4, 0, F, F), 0, 0, FILLS * F + k)

            def batch(b):
                for l in range(PAIRS):
                    slot(b, l)

            over_batches(pe, batch)
            transposes(NB - 1, PAIRS)
            values(NB - 1, PAIRS)
            values(NB - 1, PAIRS + 1)
            context_transposes(NB - 1, 37, PAIRS // 4 * NB)
            pe.wait_ge(turned_lo, items(NB - 1, 37))
            for k in range(2):
                fill(("y", k), NB - 1, 0, fills_before(NB - 1, PAIRS) + k)


_INS = ['L0_attn_x', 'L0_attn_qkv_w', 'L0_attn_out_w', 'L0_attn_bias_p', 'L0_attn_bias_a', 'L0_attn_rope_freqs',
        'L0_ffn_Wg', 'L0_ffn_w1', 'L0_ffn_w2']
_OUTS = [((8, 512, 256), 'float32')]


def kernel(**inputs):
    import numpy as _np
    import concourse.bacc as _bacc
    from concourse import mybir as _mybir
    from concourse.bass_utils import run_bass_kernel_spmd as _run

    nc = _bacc.Bacc("TRN2", target_bir_lowering=False, num_devices=1)
    arrays, args = {}, []
    for name in _INS:
        a = _np.ascontiguousarray(inputs[name])
        arrays[f"in_{name}_dram"] = a
        args.append(nc.dram_tensor(f"in_{name}_dram", a.shape, _mybir.dt.from_np(a.dtype), kind="ExternalInput").ap())
    for i, (shape, dtype) in enumerate(_OUTS):
        dt = _mybir.dt.from_np(_np.dtype(dtype))
        args.append(nc.dram_tensor(f"out_{i}_dram", shape, dt, kind="ExternalOutput").ap())
    layer(nc, *args)
    r = _run(nc, [arrays], core_ids=[0])
    got = tuple(r.results[0][f"out_{i}_dram"] for i in range(len(_OUTS)))
    return got[0]
```

```python
from contextlib import ExitStack

import concourse.bass as bass
from concourse import mybir

F32 = mybir.dt.float32
F16 = mybir.dt.float16
I32 = mybir.dt.int32
U32 = mybir.dt.uint32
ALU = mybir.AluOpType
ACT = mybir.ActivationFunctionType
AX_X = mybir.AxisListType.X

P = 128
BANK = 512
NB, S, M = 8, 512, 256
H, D = 16, 64
E, F, C = 16, 1024, 256
TOK = NB * S
NT = TOK // P
TPB = S // P
KT = M // P
NG, HG = 4, 4
SW = S + (TPB - 1) * P
EPS = 1e-5
TWO_PI_PARTS = (6.28125, 0.0019340515136718750, 1.2554228305816650e-06, 3.8192e-10)
INV_TWO_PI = 0.15915494309189535
PI_BELOW = 3.1415925
ROUND = 12582912.0
P_SCALE = 16384.0
PAIRS = NG * HG * TPB // 2
EARLY_SCATTERS = 24
FILLS = 6


def dve_linker(dve, sem):
    count = [0]

    def link(ins):
        count[0] += 1
        ins.then_inc(sem, 1)
        dve.wait_ge(sem, count[0])

    return link


def power_of_two(link, nc, n2, tmp, scale, inverse):
    link(nc.vector.tensor_scalar(tmp, n2.bitcast(I32), 23, None, ALU.logical_shift_right))
    link(nc.vector.tensor_scalar(tmp, tmp, 1, None, ALU.add))
    link(nc.vector.tensor_scalar(tmp, tmp, 1, None, ALU.logical_shift_right))
    link(nc.vector.tensor_scalar(tmp, tmp, -1, 201, ALU.mult, ALU.add))
    link(nc.vector.tensor_scalar(tmp, tmp, 167, None, ALU.min))
    link(nc.vector.tensor_scalar(scale.bitcast(I32), tmp, 23, None, ALU.logical_shift_left))
    link(nc.vector.tensor_scalar(tmp, tmp, -1, 254, ALU.mult, ALU.add))
    link(nc.vector.tensor_scalar(inverse.bitcast(I32), tmp, 23, None, ALU.logical_shift_left))


def layer(nc, x, qkv_w, out_w, bias_p, bias_a, rope_freqs, wg, w1, w2, out):
    x_tiles = x.rearrange("b (t p) m -> p (b t) m", p=P)
    xt_dram = nc.dram_tensor("xt_dram", (NB, P, 2 * KT * S), F16, kind="Internal").ap()
    slots_dram = nc.dram_tensor("slots_dram", (E * C, M), F32, kind="Internal").ap()
    expert_dram = nc.dram_tensor("expert_dram", (E * C, M), F32, kind="Internal").ap()
    source_dram = nc.dram_tensor("source_dram", (NB, P, TPB), U32, kind="Internal").ap()
    gate_dram = nc.dram_tensor("gate_dram", (NB, P, TPB), F32, kind="Internal").ap()

    with ExitStack() as whole:
        def keep(name, shape, dt=F32):
            return whole.enter_context(nc.sbuf_tensor(name, shape, dt))

        def sem(name):
            return whole.enter_context(nc.semaphore(name))

        ident = keep("ident", [P, P])
        wt = [keep(f"wqkv_{n}", [P, KT, 3 * H * D], F16) for n in ("hi", "lo")]
        wot = [keep(f"wout_{n}", [P, H * D // P, M], F16) for n in ("hi", "lo")]
        cos = keep("cos", [P, S])
        sin = keep("sin", [P, S])
        scale = keep("scale", [P, 2])
        inverse = keep("inverse", [P, 2])
        score_scale = keep("score_scale", [P, 1])
        y_scale = keep("y_scale", [P, 1])
        coef = keep("coef", [P, H])
        slope = keep("slope", [P, H])
        strips = keep("strips", [P, H, SW])
        xcur = keep("xcur", [P, 2, KT, S], F16)
        x_loaded = sem("x_loaded")
        with ExitStack() as early:
            raw = early.enter_context(nc.sbuf_tensor("raw", [P, 2, 2, 2048], F32))
            xa = early.enter_context(nc.sbuf_tensor("xa", [P, NT, M], F32))
            scatter_to = early.enter_context(nc.sbuf_tensor("scatter_to", [P, NT], U32))
            scattered = sem("scattered")
            ld_we = [[sem(f"ld_w{w + 1}_{r}") for w in range(2)] for r in range(2)]
            prepare(nc, sem, x_tiles, qkv_w, out_w, bias_p, bias_a, rope_freqs, wg, w1, w2, xt_dram, slots_dram,
                    source_dram, gate_dram, ident, wt, wot, cos, sin, scale, inverse, score_scale, y_scale, coef,
                    slope, strips, raw, xa, scatter_to, scattered, ld_we)
            experts(nc, sem, w1, w2, slots_dram, expert_dram, ident, raw, xa, scatter_to, scattered, ld_we, xt_dram, xcur, x_loaded)
        attention(nc, sem, x, out, xt_dram, xcur, x_loaded, expert_dram, source_dram, gate_dram, ident, wt, wot, cos, sin,
                  score_scale, y_scale, strips)


def scatter(nc, slots_dram, scatter_to, xa, t):
    return nc.gpsimd.indirect_dma_start(
        slots_dram[:, :], bass.IndirectOffsetOnAxis(ap=scatter_to[:, t:t + 1], axis=0), xa[:, t, :], None,
        bounds_check=E * C - 1, oob_is_err=False)


def load_expert(eng, raw, w, w1, w2, e, r, loaded):
    if w == 0:
        eng.dma_start(raw[:, r, 0, :].rearrange("p (k f) -> p k f", k=KT),
                      w1[e].rearrange("(k p) f -> p k f", p=P)).then_inc(loaded, 16)
    else:
        eng.dma_start(raw[:, r, 1, :].rearrange("p (t m) -> p t m", m=M),
                      w2[e].rearrange("(t p) m -> p t m", p=P)).then_inc(loaded, 16)


def prepare(nc, sem, x_tiles, qkv_w, out_w, bias_p, bias_a, rope_freqs, wg, w1, w2, xt_dram, slots_dram,
            source_dram, gate_dram, ident, wt, wot, cos, sin, scale, inverse, score_scale, y_scale, coef,
            slope, strips, raw, xa, scatter_to, scattered, ld_we):
    GROUPS = 4
    GT = NT // GROUPS
    with ExitStack() as ctx:
        def sb(name, shape, dt=F32):
            return ctx.enter_context(nc.sbuf_tensor(name, shape, dt))

        flat = raw[:].rearrange("p r w n -> p (r w n)")
        wraw = flat[:, 0:3 * H * D * M // P].rearrange("p (t m) -> p t m", m=M)
        wo_raw = flat[:, 3 * H * D * M // P:].rearrange("p (t n) -> p t n", n=H * D)
        junk = strips[:, H - 3:H, :].rearrange("p h s -> p (h s)")[:, 0:2048]
        gather_from = sb("gather_from", [P, NT], U32)
        gate = sb("gate", [P, NT])
        wg_sb = sb("wg_sb", [P, KT, E])
        zeros = sb("zeros", [P, M])
        ones = sb("ones", [P, P])
        onesh = sb("onesh", [P, P], F16)
        before = sb("before", [P, P], F16)
        stats = sb("stats", [P, NT, 6])
        moments = sb("moments", [P, NT, 2])
        sd = sb("sd", [P, 4, NT])
        eps = sb("eps", [P, 1])
        freq = sb("freq", [P, 1])
        wsq = sb("wsq", [P, 4])
        n2 = sb("n2", [P, 2])
        expo = sb("expo", [P, 2], I32)
        pos = sb("pos", [P, S], I32)
        ang = sb("ang", [P, S])
        turns = sb("turns", [P, S])
        xt32 = sb("xt32", [P, 2, KT, S])
        xth = sb("xth", [P, 2, 2, KT, S], F16)
        iota_e = sb("iota_e", [P, NT, E], I32)
        lanes = sb("lanes", [P, NT, E])
        rt = sb("rt", [P, 6, NT * E])
        onehot = sb("onehot", [P, NT * E], F16)
        col = sb("col", [P, 8, NT])
        raw_p = sb("raw_p", [P, H])
        psx = [ctx.enter_context(nc.psum_tensor(f"psx{i}", [P, KT, S], F32)) for i in range(2)]
        psw = [ctx.enter_context(nc.psum_tensor(f"psw{i}", [P, BANK], F32)) for i in range(2)]
        psg = ctx.enter_context(nc.psum_tensor("psg", [P, BANK], F32))
        psn = ctx.enter_context(nc.psum_tensor("psn", [P, BANK], F32))

        bank_of = [psw[0][:], psw[1][:], psx[0][:, 0, :], psx[0][:, 1, :], psx[1][:, 0, :], psx[1][:, 1, :]]
        ld_small, ld_w = sem("ld_small"), sem("ld_w")
        ld_x = [sem(f"ld_x{b}") for b in range(NB)]
        xt_stored = [sem(f"xt_stored{r}") for r in range(2)]
        const_ready, chain, pool_chain = sem("const_ready"), sem("chain_a"), sem("pool_chain_a")
        sq_done, n2_ready, scale_ready = sem("sq_done"), sem("n2_ready"), sem("scale_ready")
        var_ready, sd_ready, xn_ready = sem("var_ready"), sem("sd_ready"), sem("xn_ready")
        xt_ps, xt_hi, xt_lo, xt_32 = sem("xt_ps"), sem("xt_hi"), sem("xt_lo"), sem("xt_32")
        w_ps, w_hi, w_lo = sem("w_ps"), sem("w_hi"), sem("w_lo")
        logits_ready, shifted, exps = sem("logits_ready"), sem("shifted"), sem("exps")
        onehot_ready, counts_ready, routed = sem("onehot_ready"), sem("counts_ready"), sem("routed")
        ang_ready, sin_ready = sem("ang_ready"), sem("sin_ready")
        dist_ready, ln_ready, strips_ready = sem("dist_ready"), sem("ln_ready"), sem("strips_ready")
        routes_stored, rstd_ready = sem("routes_stored"), sem("rstd_ready")
        slope_ready, coef_ready = sem("slope_ready"), sem("coef_ready")
        xn_pool = sem("xn_pool")
        zero_ready, slots_zeroed = sem("zero_ready"), sem("slots_zeroed")
        NW = 3 * H * D // P * KT // 4
        NWO = H * D // P // 2
        logits = rt[:, 0, :].rearrange("p (t e) -> p t e", e=E)

        def r3(i):
            return rt[:, i, :].rearrange("p (t e) -> p t e", e=E)

        def spread(v):
            return v.unsqueeze(2).to_broadcast([P, NT, E])

        block = ctx.enter_context(nc.Block())

        @block.sync
        def _(sp):
            for b in range(NB):
                sp.dma_start(xa[:, b * TPB:(b + 1) * TPB, :], x_tiles[:, b * TPB:(b + 1) * TPB, :]).then_inc(ld_x[b], 16)
                if b == 0:
                    for q in range(4):
                        sp.dma_start(freq[32 * q:32 * q + 32, :], rope_freqs.unsqueeze(1)).then_inc(ld_small, 16)
                    sp.dma_start(wg_sb[:], wg.rearrange("(k p) e -> p k e", p=P)).then_inc(ld_small, 16)
                    sp.dma_start(slope[:], bias_a.rearrange("h a b -> (a b) h").to_broadcast([P, H])).then_inc(ld_small, 16)
                    sp.dma_start(raw_p[:], bias_p.rearrange("h a b -> (a b) h").to_broadcast([P, H])).then_inc(ld_small, 16)
            for b in range(NB):
                sp.wait_ge(xt_lo, b + 1)
                sp.dma_start(xt_dram[b], xth[:, b % 2].rearrange("p h k s -> p (h k s)")).then_inc(xt_stored[b % 2], 16)
                if b == 0:
                    sp.dma_start(wraw, qkv_w.rearrange("(t p) m -> p t m", p=P)).then_inc(ld_w, 16)
                elif b == 1:
                    sp.dma_start(wo_raw, out_w.rearrange("(t p) n -> p t n", p=P)).then_inc(ld_w, 16)
                    sp.wait_ge(zero_ready, 1)
                elif b < 6:
                    rows = slots_dram[(b - 2) * 1024:(b - 1) * 1024, :].rearrange("(p r) m -> p r m", p=P)
                    sp.dma_start(rows, zeros[:].unsqueeze(1).to_broadcast([P, 8, M])).then_inc(slots_zeroed, 16)
            sp.wait_ge(routed, 1)
            sp.dma_start(source_dram.rearrange("b p t -> p b t"), gather_from[:].rearrange("p (b t) -> p b t", b=NB)).then_inc(routes_stored, 16)
            sp.dma_start(gate_dram.rearrange("b p t -> p b t"), gate[:].rearrange("p (b t) -> p b t", b=NB)).then_inc(routes_stored, 16)
            sp.wait_ge(w_ps, NW + NWO)
            for r in range(2):
                for w in range(2):
                    load_expert(sp, raw, w, w1, w2, r, r, ld_we[r][w])
            for r in range(2):
                sp.wait_ge(xt_stored[r], 16 * (NB // 2))
            sp.wait_ge(slots_zeroed, 64)
            sp.wait_ge(routes_stored, 32)

        @block.gpsimd
        def _(pool):
            nc.gpsimd.memset(zeros[:], 0.0).then_inc(zero_ready, 1)
            nc.gpsimd.memset(ones[:], 1.0).then_inc(pool_chain, 1)
            nc.gpsimd.memset(onesh[:], 1.0).then_inc(pool_chain, 1)
            nc.gpsimd.memset(ident[:], 0.0).then_inc(pool_chain, 1)
            pool.wait_ge(pool_chain, 3)
            nc.gpsimd.affine_select(out=ident[:], in_=ident[:], compare_op=ALU.not_equal, fill=1.0, base=0,
                                    pattern=[[-1, P]], channel_multiplier=1).then_inc(const_ready, 1)
            nc.gpsimd.affine_select(out=before[:], in_=onesh[:], compare_op=ALU.is_gt, fill=0.0, base=0,
                                    pattern=[[1, P]], channel_multiplier=-1).then_inc(const_ready, 1)
            nc.gpsimd.iota(pos[:], pattern=[[1, S]], base=0, channel_multiplier=0).then_inc(const_ready, 1)
            nc.gpsimd.iota(iota_e[:], pattern=[[0, NT], [1, E]], base=0, channel_multiplier=0).then_inc(const_ready, 1)
            nc.gpsimd.iota(strips[:, 0, :].bitcast(I32), pattern=[[1, SW]], base=-(SW - S),
                           channel_multiplier=-1).then_inc(dist_ready, 1)
            for g in range(GROUPS):
                pool.wait_ge(rstd_ready, g + 1)
                for t in range(g * GT + GT - 2, g * GT + GT):
                    nc.gpsimd.tensor_scalar(xa[:, t, :], xa[:, t, :], moments[:, t, 0:1], sd[:, 1, t:t + 1],
                                            ALU.subtract, ALU.mult).then_inc(xn_pool, 1)
            pool.wait_ge(slots_zeroed, 64)
            pool.wait_ge(routed, 1)
            pool.wait_ge(xn_ready, NT - 2 * GROUPS)
            pool.wait_ge(xn_pool, 2 * GROUPS)
            for t in range(EARLY_SCATTERS):
                scatter(nc, slots_dram, scatter_to, xa, t).then_inc(scattered, 16)

        @block.scalar
        def _(act):
            def deviations(g):
                act.wait_ge(var_ready, g + 1)
                tiles = slice(g * GT, (g + 1) * GT)
                nc.scalar.activation(sd[:, 0, tiles], moments[:, tiles, 1], ACT.Sqrt, bias=eps[:, 0:1]).then_inc(sd_ready, 1)

            deviations(0)
            for b in range(NB):
                act.wait_ge(xt_ps, b + 1)
                if b >= 2:
                    act.wait_ge(logits_ready, b - 1)
                nc.scalar.copy(xt32[:, b % 2], psx[b % 2][:]).then_inc(xt_32, 1)
                if b >= 2:
                    act.wait_ge(xt_stored[b % 2], 16 * (b // 2))
                nc.scalar.copy(xth[:, b % 2, 0], psx[b % 2][:]).then_inc(xt_hi, 1)
                if b % 2 == 0 and b // 2 + 1 < GROUPS:
                    deviations(b // 2 + 1)
                if b >= 4:
                    q = b - 4
                    act.wait_ge(ld_w, 32)
                    if q:
                        act.wait_ge(sq_done, q)
                    nc.scalar.activation(junk, flat[:, q * 2048:(q + 1) * 2048], ACT.Square,
                                         accum_out=wsq[:, q:q + 1]).then_inc(sq_done, 1)
            act.wait_ge(shifted, 1)
            nc.scalar.activation(rt[:, 2, :], rt[:, 1, :], ACT.Exp).then_inc(exps, 1)
            act.wait_ge(ang_ready, 1)
            nc.scalar.activation(sin[:], ang[:], ACT.Sin).then_inc(sin_ready, 1)
            nc.scalar.activation(cos[:], ang[:], ACT.Sin, scale=0.5).then_inc(sin_ready, 1)
            act.wait_ge(dist_ready, 2)
            act.wait_ge(slope_ready, 1)
            act.wait_ge(sq_done, 4)
            for i in range(H):
                h = (i + 1) % H
                nc.scalar.activation(strips[:, h, :], strips[:, 0, :], ACT.Ln, bias=1.0,
                                     scale=slope[:, h:h + 1]).then_inc(ln_ready, 1)
            act.wait_ge(scale_ready, 1)
            for i in range(NW + NWO):
                act.wait_ge(w_ps, i + 1)
                which = 0 if i < NW else 1
                for o, v in weight_views(wt[0], wot[0], bank_of[i % 6], i, NW):
                    last = nc.scalar.activation(o, v, ACT.Copy, scale=scale[:, which:which + 1])
                last.then_inc(w_hi, 1)
            act.wait_ge(coef_ready, 1)
            for h in range(H // 2 + 1, H):
                nc.scalar.activation(strips[:, h, :], strips[:, h, :], ACT.Copy, scale=coef[:, h:h + 1]).then_inc(strips_ready, 1)

        @block.vector
        def _(dve):
            link = dve_linker(dve, chain)
            nc.vector.memset(eps[:], EPS)

            def statistics(g):
                for b in range(g * NB // GROUPS, (g + 1) * NB // GROUPS):
                    dve.wait_ge(ld_x[b], 16)
                    for t in range(b * TPB, (b + 1) * TPB):
                        last = nc.vector.bn_stats(stats[:, t, :], xa[:, t, :])
                link(last)
                for t in range(g * GT, (g + 1) * GT):
                    last = nc.vector.bn_aggr(moments[:, t, :], stats[:, t, :])
                last.then_inc(var_ready, 1)

            def normalise(g):
                tiles = slice(g * GT, (g + 1) * GT)
                y, a, b, c = (sd[:, i, tiles] for i in range(4))
                dve.wait_ge(sd_ready, g + 1)
                link(nc.vector.reciprocal(a, y))
                link(nc.vector.scalar_tensor_tensor(out=b, in0=moments[:, tiles, 1], scalar=eps[:, 0:1], in1=a, op0=ALU.add, op1=ALU.mult))
                link(nc.vector.tensor_tensor(c, y, b, ALU.add))
                link(nc.vector.tensor_scalar(c, c, 0.5, None, ALU.mult))
                nc.vector.reciprocal(a, c).then_inc(rstd_ready, 1)
                dve.wait_ge(rstd_ready, g + 1)
                for t in range(g * GT, (g + 1) * GT - 2):
                    nc.vector.tensor_scalar(xa[:, t, :], xa[:, t, :], moments[:, t, 0:1], sd[:, 1, t:t + 1],
                                            ALU.subtract, ALU.mult).then_inc(xn_ready, 1)

            def tables():
                dve.wait_ge(ld_small, 16 * 7)
                dve.wait_ge(const_ready, 4)
                nc.vector.tensor_scalar(slope[:], slope[:], 0.01, None, ALU.max).then_inc(slope_ready, 1)
                link(nc.vector.tensor_copy(ang[:], pos[:]))
                link(nc.vector.tensor_scalar(ang[:], ang[:], freq[:, 0:1], None, ALU.mult))
                link(nc.vector.tensor_scalar(turns[:], ang[:], INV_TWO_PI, None, ALU.mult))
                link(nc.vector.tensor_scalar(turns[:], turns[:], ROUND, None, ALU.add))
                link(nc.vector.tensor_scalar(turns[:], turns[:], ROUND, None, ALU.subtract))
                for part in TWO_PI_PARTS:
                    link(nc.vector.scalar_tensor_tensor(out=ang[:], in0=turns[:], scalar=-part, in1=ang[:], op0=ALU.mult, op1=ALU.add))
                nc.vector.tensor_scalar(ang[:], ang[:], PI_BELOW, -PI_BELOW, ALU.min, ALU.max).then_inc(ang_ready, 1)
                link(nc.vector.tensor_copy(strips[:, 1, :], strips[:, 0, :].bitcast(I32)))
                nc.vector.scalar_tensor_tensor(out=strips[:, 0, :], in0=strips[:, 1, :], scalar=-1.0, in1=strips[:, 1, :],
                                               op0=ALU.mult, op1=ALU.max).then_inc(dist_ready, 1)

            def transposed_low(b):
                dve.wait_ge(xt_hi, b + 1)
                nc.vector.tensor_tensor(xth[:, b % 2, 1], psx[b % 2][:], xth[:, b % 2, 0], ALU.subtract).then_inc(xt_lo, 1)

            statistics(0)
            normalise(0)
            for g in range(1, GROUPS):
                statistics(g)
                transposed_low(2 * g - 2)
                normalise(g)
                transposed_low(2 * g - 1)
            tables()
            transposed_low(NB - 2)
            transposed_low(NB - 1)
            dve.wait_ge(logits_ready, NB)
            dve.wait_ge(const_ready, 4)
            link(nc.vector.tensor_copy(rt[:, 0, :], psg[:]))
            link(nc.vector.tensor_copy(lanes[:], iota_e[:]))
            link(nc.vector.tensor_reduce(col[:, 0, :], logits, AX_X, ALU.max))
            nc.vector.tensor_tensor(r3(1), logits, spread(col[:, 0, :]), ALU.subtract).then_inc(shifted, 1)
            dve.wait_ge(n2_ready, 1)
            link(nc.vector.tensor_reduce(n2[:, 0:1], psn[:, 0:3], AX_X, ALU.add))
            link(nc.vector.tensor_copy(n2[:, 1:2], psn[:, 3:4]))
            power_of_two(link, nc, n2[:], expo[:], scale[:], inverse[:])
            nc.vector.tensor_tensor(score_scale[:], inverse[:, 0:1], inverse[:, 0:1], ALU.mult).then_inc(scale_ready, 1)
            dve.wait_ge(scale_ready, 1)
            link(nc.vector.tensor_scalar(score_scale[:], score_scale[:], -float(D) ** -0.5, None, ALU.mult))
            link(nc.vector.tensor_tensor(y_scale[:], inverse[:, 0:1], inverse[:, 1:2], ALU.mult))
            link(nc.vector.tensor_scalar(coef[:], raw_p[:], 0.01, None, ALU.max))
            link(nc.vector.tensor_scalar(coef[:], coef[:], -float(D) ** 0.5, None, ALU.mult))
            nc.vector.tensor_scalar(coef[:], coef[:], scale[:, 0:1], scale[:, 0:1], ALU.mult, ALU.mult).then_inc(coef_ready, 1)
            dve.wait_ge(coef_ready, 1)
            dve.wait_ge(exps, 1)
            link(nc.vector.tensor_reduce(col[:, 1, :], r3(2), AX_X, ALU.add))
            link(nc.vector.reciprocal(col[:, 2, :], col[:, 1, :]))
            link(nc.vector.tensor_scalar(r3(3), r3(1), 0.0, -float(E), ALU.is_ge, ALU.mult))
            link(nc.vector.tensor_tensor(r3(3), r3(3), lanes[:], ALU.add))
            link(nc.vector.tensor_reduce(col[:, 3, :], r3(3), AX_X, ALU.min))
            link(nc.vector.tensor_scalar(col[:, 3, :], col[:, 3, :], float(E), None, ALU.add))
            link(nc.vector.tensor_tensor(r3(4), lanes[:], spread(col[:, 3, :]), ALU.is_equal))
            nc.vector.tensor_copy(onehot[:], rt[:, 4, :]).then_inc(onehot_ready, 1)
            dve.wait_ge(counts_ready, 2)
            link(nc.vector.tensor_copy(rt[:, 1, :], psn[:]))
            link(nc.vector.tensor_copy(rt[:, 5, :], psg[:]))
            src, dst, step = 1, 2, 1
            while step < NT:
                w = step * E
                link(nc.vector.tensor_copy(rt[:, dst, 0:w], rt[:, src, 0:w]))
                link(nc.vector.tensor_tensor(rt[:, dst, w:], rt[:, src, w:], rt[:, src, 0:NT * E - w], ALU.add))
                src, dst = dst, (3 if dst == 2 else 2)
                step *= 2
            link(nc.vector.tensor_tensor(rt[:, src, :], rt[:, src, :], rt[:, 1, :], ALU.subtract))
            link(nc.vector.tensor_tensor(rt[:, src, :], rt[:, src, :], rt[:, 5, :], ALU.add))
            link(nc.vector.tensor_tensor(rt[:, src, :], rt[:, src, :], rt[:, 4, :], ALU.mult))
            link(nc.vector.tensor_reduce(col[:, 4, :], r3(src), AX_X, ALU.add))
            link(nc.vector.tensor_scalar(col[:, 5, :], col[:, 3, :], float(C), None, ALU.mult))
            link(nc.vector.tensor_scalar(col[:, 6, :], col[:, 4, :], float(C), None, ALU.is_ge))
            link(nc.vector.scalar_tensor_tensor(out=col[:, 7, :], in0=col[:, 6, :], scalar=float(2 * E * C), in1=col[:, 4, :], op0=ALU.mult, op1=ALU.add))
            link(nc.vector.tensor_tensor(scatter_to[:], col[:, 7, :], col[:, 5, :], ALU.add))
            link(nc.vector.scalar_tensor_tensor(out=gather_from[:], in0=col[:, 4, :], scalar=float(C - 1), in1=col[:, 5, :], op0=ALU.min, op1=ALU.add))
            link(nc.vector.tensor_scalar(col[:, 6, :], col[:, 6, :], -1.0, 1.0, ALU.mult, ALU.add))
            nc.vector.tensor_tensor(gate[:], col[:, 6, :], col[:, 2, :], ALU.mult).then_inc(routed, 1)
            dve.wait_ge(sin_ready, 2)
            link(nc.vector.tensor_tensor(cos[:], cos[:], cos[:], ALU.mult))
            link(nc.vector.tensor_scalar(cos[:], cos[:], -2.0, 1.0, ALU.mult, ALU.add))
            for i in range(NW + NWO):
                dve.wait_ge(w_hi, i + 1)
                which = 0 if i < NW else 1
                for (o, v), (h, _) in zip(weight_views(wt[1], wot[1], bank_of[i % 6], i, NW), weight_views(wt[0], wot[0], bank_of[i % 6], i, NW)):
                    last = nc.vector.scalar_tensor_tensor(out=o, in0=v, scalar=scale[:, which:which + 1], in1=h,
                                                          op0=ALU.mult, op1=ALU.subtract)
                last.then_inc(w_lo, 1)
            dve.wait_ge(ln_ready, H)
            for h in range(H // 2 + 1):
                nc.vector.tensor_scalar(strips[:, h, :], strips[:, h, :], coef[:, h:h + 1], None, ALU.mult).then_inc(strips_ready, 1)
            dve.wait_ge(strips_ready, H)

        @block.tensor
        def _(pe):
            def logits_of(b):
                pe.wait_ge(xt_32, b + 1)
                for t in range(TPB):
                    n = b * TPB + t
                    for k in range(KT):
                        last = nc.tensor.matmul(psg[:, n * E:(n + 1) * E], xt32[:, b % 2, k, t * P:(t + 1) * P],
                                                wg_sb[:, k, :], start=(k == 0), stop=(k == KT - 1))
                last.then_inc(logits_ready, 1)

            pe.wait_ge(const_ready, 1)
            pe.wait_ge(ld_small, 16 * 7)
            for b in range(NB):
                if b >= 2:
                    pe.wait_ge(xt_lo, b - 1)
                g = b * TPB // GT
                pe.wait_ge(xn_ready, g * (GT - 2) + (TPB if b % 2 == 0 else GT - 2))
                if b % 2:
                    pe.wait_ge(xn_pool, 2 * g + 2)
                for k in range(KT):
                    for t in range(TPB):
                        last = nc.tensor.transpose(psx[b % 2][:, k, t * P:(t + 1) * P],
                                                   xa[:, b * TPB + t, k * P:(k + 1) * P], ident[:])
                last.then_inc(xt_ps, 1)
                if b:
                    logits_of(b - 1)
            logits_of(NB - 1)
            pe.wait_ge(sq_done, 4)
            nc.tensor.matmul(psn[:, 0:4], ones[:], wsq[:], start=True, stop=True).then_inc(n2_ready, 1)
            pe.wait_ge(onehot_ready, 1)
            pe.wait_ge(const_ready, 2)
            nc.tensor.matmul(psg[:], before[:], onehot[:], start=True, stop=True).then_inc(counts_ready, 1)
            nc.tensor.matmul(psn[:], onesh[:], onehot[:], start=True, stop=True).then_inc(counts_ready, 1)
            for i in range(NW + NWO):
                if i == 2:
                    pe.wait_ge(xt_lo, NB)
                if i >= 6:
                    pe.wait_ge(w_lo, i - 5)
                for q in range(4):
                    if i < NW:
                        k, t = i // (NW // KT), 4 * (i % (NW // KT)) + q
                        src = wraw[:, t, k * P:(k + 1) * P]
                    else:
                        k, t = 2 * (i - NW) + q // 2, q % 2
                        src = wo_raw[:, t, k * P:(k + 1) * P]
                    last = nc.tensor.transpose(bank_of[i % 6][:, q * P:(q + 1) * P], src, ident[:])
                last.then_inc(w_ps, 1)


def weight_views(w, wo, bank, i, nw):
    if i >= nw:
        k = 2 * (i - nw)
        return [(wo[:, k:k + 2, :], bank.rearrange("p (k n) -> p k n", k=2))]
    per = nw // KT
    k, c = i // per, i % per * BANK
    if c >= 2 * H * D:
        return [(w[:, k, c:c + BANK], bank)]
    found = []
    for g in range(2):
        a = c + g * HG * D
        for f in range(2):
            found.append((w[:, k, a + f * P:a + (f + 1) * P].rearrange("p (h j) -> p h j", h=HG),
                          bank[:, g * HG * D:(g + 1) * HG * D].rearrange("p (h f j) -> p h f j", h=HG, f=2)[:, :, f, :]))
    return found


def experts(nc, sem, w1, w2, slots_dram, expert_dram, ident, raw, xa, scatter_to, scattered, ld_w, xt_dram, xcur, x_loaded):
    FT = F // P
    CT = C // P
    SCALING = 10
    with ExitStack() as ctx:
        def sb(name, shape, dt=F32):
            return ctx.enter_context(nc.sbuf_tensor(name, shape, dt))

        whi = sb("whi", [P, 2, 2, 2048], F16)
        wlo = sb("wlo", [P, 2, 2, 2048], F16)
        xa_flat, xa_half = xa[:].rearrange("p t m -> p (t m)"), xa[:].rearrange("p t m -> p (t m)").bitcast(F16)
        n_rows, n_hid, n_dt = 2 * CT * M, 4 * FT * C, 4 * KT * C
        rows = xa_flat[:, 0:n_rows].rearrange("p (r t m) -> p r t m", r=2, t=CT)
        eo = xa_flat[:, n_rows:2 * n_rows].rearrange("p (r t m) -> p r t m", r=2, t=CT)
        at = 4 * n_rows
        dt = xa_half[:, at:at + n_dt].rearrange("p (r a k c) -> p r a k c", r=2, a=2, k=KT)
        hid = xa_half[:, at + n_dt:at + n_dt + n_hid].rearrange("p (r a f c) -> p r a f c", r=2, a=2, f=FT)
        junk = sb("junk_e", [P, 2048])
        wsq = sb("wsq_e", [P, 2, 2])
        n2 = sb("n2_e", [P, 2])
        expo = sb("expo_e", [P, 2], I32)
        scale = sb("scale_e", [P, 2, 2])
        inverse = sb("inverse_e", [P, 2])
        un = sb("un_e", [P, 2, 1])
        onesf = sb("ones_e", [P, P])
        psd = ctx.enter_context(nc.psum_tensor("psd", [P, KT, C], F32))
        psh = [ctx.enter_context(nc.psum_tensor(f"psh{i}", [P, BANK], F32)) for i in range(4)]
        pso = [ctx.enter_context(nc.psum_tensor(f"pso{i}", [P, CT, M], F32)) for i in range(2)]
        psn = ctx.enter_context(nc.psum_tensor("psn_e", [P, BANK], F32))

        ld_rows = [sem(f"ld_rows{r}") for r in range(2)]
        ones_ready = sem("ones_e_ready")
        sq_done, n2_ready = sem("sq_e"), sem("n2_e_ready")
        scaling = sem("scaling")
        w1_hi, w2_hi = sem("w1_hi"), sem("w2_hi")
        w1_lo, w2_lo = sem("w1_lo"), sem("w2_lo")
        d_ps, d_hi, d_lo = sem("d_ps"), sem("d_hi"), sem("d_lo")
        h_ps, h_hi, h_lo = sem("h_ps"), sem("h_hi"), sem("h_lo")
        o_ps, o_sb = sem("o_ps"), sem("o_sb")
        o_stored = [sem(f"o_stored{r}") for r in range(2)]
        block = ctx.enter_context(nc.Block())
        rows_v = slots_dram.rearrange("(e t p) m -> e p t m", p=P, t=CT)
        eo_v = expert_dram.rearrange("(e t p) m -> e p t m", p=P, t=CT)

        went_on = sem("went_on_e")

        def over_experts(eng, one, lead=0):
            for n in range(-lead, 1):
                one(n, 0)
                one(n, 1)
            with eng.Fori(1, E // 2 - 1) as n:
                one(n, 0)
                one(n, 1)
            one(E // 2 - 1, 0)
            one(E // 2 - 1, 1)

        def there(e):
            return not isinstance(e, int) or 0 <= e < E

        def wait(eng, s, v):
            if not isinstance(v, int) or v > 0:
                eng.wait_ge(s, v)

        @block.sync
        def _(sp):
            def load(n, r):
                e = 2 * n + r
                first = isinstance(e, int) and e < 2
                if not first:
                    sp.wait_ge(w1_lo, 2 * e - 2)
                    sp.sem_inc(went_on)
                    load_expert(sp, raw, 0, w1, w2, e, r, ld_w[r][0])
                    sp.wait_ge(d_ps, e - 1)
                    sp.sem_inc(went_on)
                if isinstance(e, int) and e == 0:
                    sp.wait_ge(scattered, 16 * NT)
                sp.dma_start(rows[:, r], rows_v[e]).then_inc(ld_rows[r], 16)
                if not first:
                    sp.wait_ge(w2_lo, 2 * e - 2)
                    sp.sem_inc(went_on)
                    load_expert(sp, raw, 1, w1, w2, e, r, ld_w[r][1])

            over_experts(sp, load)
            sp.dma_start(xcur[:].rearrange("p h k s -> p (h k s)"), xt_dram[0]).then_inc(x_loaded, 16)

        @block.gpsimd
        def _(pool):
            nc.gpsimd.memset(onesf[:], 1.0).then_inc(ones_ready, 1)
            for t in range(EARLY_SCATTERS, NT):
                scatter(nc, slots_dram, scatter_to, xa, t).then_inc(scattered, 16)

            def store(n, r):
                e = 2 * n + r
                pool.wait_ge(o_sb, e + 1)
                pool.dma_start(eo_v[e], eo[:, r]).then_inc(o_stored[r], 16)

            over_experts(pool, store)
            for r in range(2):
                pool.wait_ge(o_stored[r], 16 * (E // 2))

        @block.scalar
        def _(act):
            def w2_high(n, r, half):
                e = 2 * n + r
                if half == 0:
                    act.wait_ge(scaling, SCALING * (e + 1))
                    wait(act, o_ps, e - 1)
                cols = slice(half * 1024, half * 1024 + 1024)
                nc.scalar.activation(whi[:, r, 1, cols], raw[:, r, 1, cols], ACT.Copy, scale=scale[:, r, 1:2]).then_inc(w2_hi, 1)

            def hidden(n, r, q):
                e = 2 * n + r
                if q == 0:
                    wait(act, o_ps, e - 1)
                act.wait_ge(h_ps, 4 * e + q + 1)
                nc.scalar.activation(hid[:, r, 0, 2 * q:2 * q + 2, :], psh[q][:].rearrange("p (f c) -> p f c", f=2), ACT.Relu).then_inc(h_hi, 1)

            def rows_high(n, r):
                e = 2 * n + r
                wait(act, h_ps, 4 * e - 4)
                act.wait_ge(d_ps, e + 1)
                nc.scalar.copy(dt[:, r, 0], psd[:]).then_inc(d_hi, 1)

            def squares(n, r):
                e = 2 * n + r
                wait(act, n2_ready, e - 1)
                for w in range(2):
                    act.wait_ge(ld_w[r][w], 16 * n + 16)
                    wait(act, sq_done, 2 * e + w)
                    nc.scalar.activation(junk[:], raw[:, r, w, :], ACT.Square, accum_out=wsq[:, r, w:w + 1]).then_inc(sq_done, 1)

            def rows_out(n, r):
                e = 2 * n + r
                act.wait_ge(o_ps, e + 1)
                wait(act, o_stored[r], 16 * n)
                nc.scalar.activation(eo[:, r], pso[r][:], ACT.Copy, scale=un[:, r, 0:1]).then_inc(o_sb, 1)

            def one(n, r):
                e = 2 * n + r
                for q in range(4):
                    if there(e):
                        hidden(n, r, q)
                    if q < 2 and there(e + 1):
                        w2_high(n + r, 1 - r, q)
                before_rows = isinstance(e, int) and e < 0
                if before_rows:
                    squares(n + 1, r)
                if there(e + 1):
                    rows_high(n + r, 1 - r)
                if there(e + 2) and not before_rows:
                    squares(n + 1, r)
                if there(e):
                    rows_out(n, r)

            over_experts(act, one, lead=1)

        @block.vector
        def _(dve):
            def scales(n, r):
                e = 2 * n + r
                c = [0]

                def link(ins):
                    c[0] += 1
                    ins.then_inc(scaling, 1)
                    dve.wait_ge(scaling, e * SCALING + c[0])

                dve.wait_ge(n2_ready, e + 1)
                link(nc.vector.tensor_copy(n2[:], psn[:, 0:2]))
                wait(dve, w2_hi, 2 * e - 2)
                power_of_two(link, nc, n2[:], expo[:], scale[:, r, :], inverse[:])
                wait(dve, o_sb, e - 1)
                link(nc.vector.tensor_tensor(un[:, r, :], inverse[:, 0:1], inverse[:, 1:2], ALU.mult))
                assert c[0] == SCALING

            def w1_high(n, r):
                e = 2 * n + r
                wait(dve, h_ps, 4 * e - 4)
                nc.vector.tensor_scalar(whi[:, r, 0, :], raw[:, r, 0, :], scale[:, r, 0:1], None, ALU.mult).then_inc(w1_hi, 1)

            def weight_low(n, r, w, half):
                e = 2 * n + r
                if half == 0:
                    if w == 0:
                        dve.wait_ge(w1_hi, e + 1)
                    else:
                        dve.wait_ge(w2_hi, 2 * e + 2)
                cols = slice(half * 1024, (half + 1) * 1024)
                nc.vector.scalar_tensor_tensor(out=wlo[:, r, w, cols], in0=raw[:, r, w, cols], scalar=scale[:, r, w:w + 1],
                                               in1=whi[:, r, w, cols], op0=ALU.mult, op1=ALU.subtract).then_inc((w1_lo, w2_lo)[w], 1)

            def rows_low(n, r):
                dve.wait_ge(d_hi, 2 * n + r + 1)
                nc.vector.tensor_tensor(dt[:, r, 1], psd[:], dt[:, r, 0], ALU.subtract).then_inc(d_lo, 1)

            def hidden_low(n, r, q):
                dve.wait_ge(h_hi, 4 * (2 * n + r) + q + 1)
                nc.vector.scalar_tensor_tensor(out=hid[:, r, 1, 2 * q:2 * q + 2, :], in0=psh[q][:].rearrange("p (f c) -> p f c", f=2), scalar=0.0,
                                               in1=hid[:, r, 0, 2 * q:2 * q + 2, :], op0=ALU.max, op1=ALU.subtract).then_inc(h_lo, 1)

            def one(n, r):
                e = 2 * n + r
                nxt = (n + r, 1 - r)
                if there(e + 1):
                    scales(*nxt)
                    w1_high(*nxt)
                for q in range(4):
                    if there(e):
                        hidden_low(n, r, q)
                    if q == 1 and there(e + 1):
                        weight_low(*nxt, 0, 0)
                before_rows = isinstance(e, int) and e < 0
                if there(e + 1) and not before_rows:
                    rows_low(*nxt)
                if there(e + 1):
                    weight_low(*nxt, 0, 1)
                    weight_low(*nxt, 1, 0)
                    weight_low(*nxt, 1, 1)
                if there(e + 1) and before_rows:
                    rows_low(*nxt)

            over_experts(dve, one, lead=1)

        @block.tensor
        def _(pe):
            PARTS = ((0, 0), (0, 1), (1, 0))
            split = (whi, wlo)
            pe.wait_ge(ones_ready, 1)

            def turn_rows(n, r):
                e = 2 * n + r
                pe.wait_ge(ld_rows[r], 16 * n + 16)
                wait(pe, d_lo, e)
                for k in range(KT):
                    for t in range(CT):
                        last = nc.tensor.transpose(psd[:, k, t * P:(t + 1) * P], rows[:, r, t, k * P:(k + 1) * P], ident[:])
                last.then_inc(d_ps, 1)

            def norms(n, r):
                e = 2 * n + r
                pe.wait_ge(sq_done, 2 * e + 2)
                wait(pe, scaling, SCALING * e)
                nc.tensor.matmul(psn[:, 0:2], onesf[:], wsq[:, r, :], start=True, stop=True).then_inc(n2_ready, 1)

            def hidden(n, r):
                e = 2 * n + r
                pe.wait_ge(w1_lo, 2 * e + 2)
                pe.wait_ge(d_lo, e + 1)
                for q in range(4):
                    wait(pe, h_lo, 4 * e + q - 3)
                    for f in range(2):
                        m = 0
                        for k in range(KT):
                            for a, b in PARTS:
                                fc = k * F + (2 * q + f) * P
                                last = nc.tensor.matmul(psh[q][:, f * C:(f + 1) * C], split[a][:, r, 0, fc:fc + P],
                                                        dt[:, r, b, k, :], start=(m == 0), stop=(m == 3 * KT - 1))
                                m += 1
                    last.then_inc(h_ps, 1)

            def rows_out(n, r):
                e = 2 * n + r
                pe.wait_ge(w2_lo, 2 * e + 2)
                wait(pe, o_sb, e - 1)
                for t in range(CT):
                    m = 0
                    for f in range(FT):
                        if t == 0 and f % 2 == 0:
                            pe.wait_ge(h_lo, 4 * e + f // 2 + 1)
                        for a, b in PARTS:
                            last = nc.tensor.matmul(pso[r][:, t, :], hid[:, r, a, f, t * P:(t + 1) * P],
                                                    split[b][:, r, 1, f * M:(f + 1) * M], start=(m == 0), stop=(m == 3 * FT - 1))
                            m += 1
                last.then_inc(o_ps, 1)

            def one(n, r):
                e = 2 * n + r
                if there(e):
                    hidden(n, r)
                before_rows = isinstance(e, int) and e < 0
                if before_rows:
                    norms(n + 1, r)
                if there(e + 1):
                    turn_rows(n + r, 1 - r)
                if there(e):
                    rows_out(n, r)
                if there(e + 2) and not before_rows:
                    norms(n + 1, r)

            over_experts(pe, one, lead=1)


def attention(nc, sem, x, out, xt_dram, xcur, x_loaded, expert_dram, source_dram, gate_dram, ident, wt, wot, cos, sin,
              score_scale, y_scale, strips):
    with ExitStack() as ctx:
        def sb(name, shape, dt=F32):
            return ctx.enter_context(nc.sbuf_tensor(name, shape, dt))

        proj = sb("proj", [P, 2, 2, S])
        prod = sb("prod", [P, 4, S])
        rot = sb("rot", [P, 2, 2, S])
        parts = sb("parts", [P, 2, 2, 2, S], F16)
        qk = sb("qk", [P, 2, 2, HG, S], F16)
        kswap = sb("kswap", [P, 2, HG, S], F16)
        val = [sb(f"val_{n}", [P, 4, TPB, HG * D], F16) for n in ("hi", "lo")]
        neg = sb("neg", [P, 2, 2, S])
        neg_max = sb("neg_max", [P, 4])
        prob = sb("prob", [P, 2, 2, S])
        sums = sb("sums", [P, 2, 8])
        rsum = sb("rsum", [P, 8])
        pt = [sb(f"pt_{n}", [P, 2, 2, TPB, P], F16) for n in ("hi", "lo")]
        ctxt = sb("ctxt", [P, TPB, HG * D])
        ot = [sb(f"ot_{n}", [P, 2, S], F16) for n in ("hi", "lo")]
        yacc = sb("yacc", [P, TPB, M])
        got = sb("got", [P, 2, M])
        source = sb("source", [P, TPB], U32)
        gate = sb("gate_now", [P, TPB])

        proj0, prod0 = prob, neg[:].rearrange("p r q s -> p (r q) s")
        ps_s = [ctx.enter_context(nc.psum_tensor(f"ps_s{i}", [P, BANK], F32)) for i in range(2)]
        ps_t = [ctx.enter_context(nc.psum_tensor(f"ps_t{i}", [P, 2, BANK], F32)) for i in range(2)]
        ps_o = ctx.enter_context(nc.psum_tensor("ps_o", [P, BANK], F32))
        ps_x = ctx.enter_context(nc.psum_tensor("ps_x", [P, BANK], F32))

        chain = sem("chain_c")
        residual_loaded, y_stored = sem("residual_loaded"), sem("y_stored")
        routes_loaded = sem("routes_loaded")
        gathered = [sem(f"gathered{i}") for i in range(2)]
        combined = sem("combined")
        qk_moved = [sem(f"qk_moved{r}") for r in range(2)]
        scored = sem("scored")
        negated = sem("negated")
        exp_done = sem("exp_done")
        turned, turned_hi, turned_lo = sem("turned"), sem("turned_hi"), sem("turned_lo")
        pv_done = sem("pv_done")
        ctx_read = sem("ctx_read")
        filled, x_free = sem("filled"), sem("x_free")
        val_hi = sem("val_hi")
        turned_parts = sem("rotations")
        parts_hi, parts_lo = sem("parts_hi"), sem("parts_lo")

        went_on = sem("went_on")

        FIRST_FILLS = [(F, k) for F in range(2) for k in range(4)] + [(F, k) for F in range(2) for k in (4, 5)]
        MOVED = 16 * 18

        def fills_before(b, l):
            n = 2 * FILLS + PAIRS * b + l
            n = n - (min(max(l - 6, 0), 2) if isinstance(b, int) and b == 0 else 2)
            if isinstance(b, int) and b == NB - 1:
                n -= sum(m // 8 >= 2 and m % 8 < FILLS for m in range(l))
            return n

        def pair_item(l):
            return 9 * (l // 8) + l % 8 + (l % 8 > 3)

        def items(b, n):
            if isinstance(b, int) and b == 0:
                return n + 1 - (n >= 0) - (n >= 4)
            return 36 * b + n + 1 - 2

        def wait(eng, s, v):
            if not isinstance(v, int) or v > 0:
                eng.wait_ge(s, v)

        def over_batches(eng, batch):
            batch(0)
            with eng.Fori(1, NB - 1) as b:
                batch(b)
            batch(NB - 1)

        def is_first(b):
            return isinstance(b, int) and b == 0

        def is_last(b):
            return isinstance(b, int) and b == NB - 1

        def ahead(b, j):
            if is_last(b) and j >= 2:
                return None
            return 2 * b + j // 2 + 1, j % 2, (j + 2) % 4

        def slot_kind(b, l):
            j, k = divmod(l, 8)
            if k < FILLS:
                return ahead(b, j) and ("qk" if k < 4 else "v", k if k < 4 else k - 4, *ahead(b, j))
            return None if is_first(b) and j == 0 else ("y", k - FILLS)

        def wait_parts_moved(eng, n, r):
            if r:
                eng.wait_ge(qk_moved[0], MOVED * (n + 1))
            else:
                wait(eng, qk_moved[1], MOVED * n)

        block = ctx.enter_context(nc.Block())

        @block.sync
        def _(sp):
            def move(n, r):
                F = 2 * n + r
                wait(sp, scored, 16 * (F - 1))
                sp.wait_ge(parts_lo, 2 * F + 2)
                for h in range(HG):
                    rows = slice(32 * h, 32 * h + 32)
                    for q in range(4):
                        sp.dma_start(qk[32 * q:32 * q + 32, r, :, h, :], parts[rows, q // 2, :, q % 2, :]).then_inc(qk_moved[r], 16)
                sp.wait_ge(qk_moved[r], MOVED * n + 256)
                sp.sem_inc(went_on)
                for c in (0, 64):
                    sp.dma_start(kswap[64 - c:128 - c, r], qk[c:c + 64, r, 1]).then_inc(qk_moved[r], 16)

            def load_x(b):
                sp.dma_start(xcur[:].rearrange("p h k s -> p (h k s)"), xt_dram[b]).then_inc(x_loaded, 16)

            def load_routes(b):
                wait(sp, combined, TPB * b)
                sp.sem_inc(went_on)
                sp.dma_start(source[:], source_dram[b]).then_inc(routes_loaded, 16)
                sp.dma_start(gate[:], gate_dram[b]).then_inc(routes_loaded, 16)

            def batch(b):
                load_routes(b)
                for j in range(4):
                    if j == 1 and not is_last(b):
                        sp.wait_ge(filled, fills_before(b, 14))
                        sp.sem_inc(went_on)
                        load_x(b + 1)
                    if ahead(b, j):
                        move(*ahead(b, j)[:2])

            move(0, 0)
            move(0, 1)
            over_batches(sp, batch)
            sp.wait_ge(x_free, fills_before(NB - 1, PAIRS) + 2)
            sp.dma_start(out[NB - 1].rearrange("(t p) m -> p t m", p=P), yacc[:]).then_inc(y_stored, 16)
            sp.wait_ge(y_stored, 16 * NB)

        @block.gpsimd
        def _(pool):
            def turn(F, w, n):
                done = 6 * (2 * F + w)
                pool.wait_ge(x_free, n)
                wait(pool, turned_parts, done)
                for i, (half, table) in enumerate(((0, cos), (1, sin), (0, sin), (1, cos))):
                    nc.gpsimd.tensor_tensor(prod[:, i, :], proj[:, w, half, :], table[:], ALU.mult).then_inc(turned_parts, 1)
                pool.wait_ge(turned_parts, done + 4)
                wait(pool, parts_lo, 2 * F - 1 + w)
                nc.gpsimd.tensor_tensor(rot[:, w, 0, :], prod[:, 0, :], prod[:, 1, :], ALU.subtract).then_inc(turned_parts, 1)
                nc.gpsimd.tensor_tensor(rot[:, w, 1, :], prod[:, 2, :], prod[:, 3, :], ALU.add).then_inc(turned_parts, 1)

            def step(F, fills):
                turn(F, 0, fills + 2)
                turn(F, 1, fills + 4)
                for w in range(2):
                    pool.wait_ge(parts_hi, 2 * F + w + 1)
                    nc.gpsimd.tensor_tensor(parts[:, 1, w], rot[:, w], parts[:, 0, w], ALU.subtract).then_inc(parts_lo, 1)

            def gather(b, j):
                if j == 0:
                    pool.wait_ge(routes_loaded, 32 * b + 32)
                wait(pool, combined, TPB * b + 2 * j)
                pool.sem_inc(went_on)
                for i in range(2):
                    nc.gpsimd.indirect_dma_start(
                        got[:, i, :], None, expert_dram[:, :],
                        bass.IndirectOffsetOnAxis(ap=source[:, 2 * j + i:2 * j + i + 1], axis=0),
                        bounds_check=E * C - 1, oob_is_err=False).then_inc(gathered[i], 16)

            def batch(b):
                for j in range(4):
                    if ahead(b, j):
                        n, r, _ = ahead(b, j)
                        step(2 * n + r, fills_before(b, 8 * j))
                    if j < 2:
                        gather(b, j)

            step(1, FIRST_FILLS.index((1, 0)))
            over_batches(pool, batch)

        @block.scalar
        def _(act):
            def read_fill(kind, fill, to=proj):
                what, k = kind[:2]
                if what == "y":
                    return
                n, r, _ = kind[2:]
                F = 2 * n + r
                act.wait_ge(filled, fill + 1)
                if what == "qk":
                    if to is proj and not (isinstance(F, int) and F == 1):
                        wait(act, turned_parts, 6 * (2 * F - 2 + k // 2) + 4)
                    nc.scalar.copy(to[:, k // 2, k % 2, :], ps_x[:]).then_inc(x_free, 1)
                else:
                    nc.scalar.copy(val[0][:, kind[4], 2 * k:2 * k + 2, :],
                                   ps_x[:].rearrange("p (t n) -> p t n", t=2)).then_inc(val_hi, 1)

            def high(n, r, w):
                act.wait_ge(turned_parts, 6 * (4 * n + 2 * r + w) + 6)
                wait_parts_moved(act, n, r)
                nc.scalar.copy(parts[:, 0, w], rot[:, w]).then_inc(parts_hi, 1)

            def pair_hi(b, l):
                item = pair_item(l)
                act.wait_ge(turned, items(b, item))
                wait(act, pv_done, PAIRS * b + l - 2)
                nc.scalar.activation(pt[0][:, (l - 1) % 2].rearrange("p q k c -> p q (k c)"), ps_t[item % 2][:],
                                     ACT.Copy, scale=P_SCALE).then_inc(turned_hi, 1)

            def ctx_hi(b, item):
                act.wait_ge(turned, items(b, item))
                nc.scalar.activation(ot[0][:], ps_t[item % 2][:], ACT.Copy, scale=1.0 / P_SCALE).then_inc(turned_hi, 1)

            def slot(b, l):
                s = PAIRS * b + l
                j, k = divmod(l, 8)
                kind = slot_kind(b, l)
                if kind:
                    read_fill(kind, fills_before(b, l))
                if l or not is_first(b):
                    pair_hi(b, l)
                for q in range(2):
                    act.wait_ge(negated, 2 * s + q + 1)
                    if q == 0:
                        wait(act, turned, items(b, pair_item(l - 1)))
                    nc.scalar.activation(prob[:, l % 2, q, :], neg[:, l % 2, q, :], ACT.Exp,
                                         bias=neg_max[:, 2 * (l % 2) + q:2 * (l % 2) + q + 1], scale=-1.0,
                                         accum_out=sums[:, l // 4 % 2, 2 * (l % 4) + q:2 * (l % 4) + q + 1]).then_inc(exp_done, 1)
                if k == 3 and not (is_first(b) and j == 0):
                    ctx_hi(b, 9 * j + 4)
                if k in (5, 7) and ahead(b, j):
                    high(*ahead(b, j)[:2], k // 7)
                if l == 9 and not is_first(b):
                    act.wait_ge(x_free, fills_before(b, 8))
                    act.dma_start(out[b - 1].rearrange("(t p) m -> p t m", p=P), yacc[:]).then_inc(y_stored, 16)
                if l == 11:
                    wait(act, y_stored, 16 * b)
                    act.dma_start(yacc[:], x[b].rearrange("(t p) m -> p t m", p=P)).then_inc(residual_loaded, 16)

            def fills(F, which):
                for k in which:
                    read_fill(("qk" if k < 4 else "v", k if k < 4 else k - 4, 0, F, F), FIRST_FILLS.index((F, k)),
                              (proj0, proj)[F])

            fills(0, range(4))
            fills(1, (0, 1))
            high(0, 0, 0)
            fills(1, (2, 3))
            high(0, 0, 1)
            fills(0, (4, 5))
            fills(1, (4, 5))
            high(0, 1, 0)
            high(0, 1, 1)

            def batch(b):
                for l in range(PAIRS):
                    slot(b, l)

            over_batches(act, batch)
            pair_hi(NB - 1, PAIRS)
            ctx_hi(NB - 1, 37)

        @block.vector
        def _(dve):
            def read_fill(kind, b, l, fill):
                what, k = kind[:2]
                if what == "v":
                    n, r, _ = kind[2:5]
                    dve.wait_ge(val_hi, 4 * n + 2 * r + k + 1)
                    nc.vector.tensor_tensor(val[1][:, kind[4], 2 * k:2 * k + 2, :], ps_x[:].rearrange("p (t n) -> p t n", t=2),
                                            val[0][:, kind[4], 2 * k:2 * k + 2, :], ALU.subtract).then_inc(x_free, 1)
                elif what == "y":
                    dve.wait_ge(filled, fill + 1)
                    if l // 8 == 1:
                        dve.wait_ge(residual_loaded, 16 * b + 16)
                    if l == 14 or l == 31:
                        dve.wait_ge(combined, TPB * b + 2 + 2 * k)
                    part = yacc[:, 2 * k:2 * k + 2, :].rearrange("p t m -> p (t m)")
                    nc.vector.scalar_tensor_tensor(out=part, in0=ps_x[:], scalar=y_scale[:, 0:1], in1=part,
                                                   op0=ALU.mult, op1=ALU.add).then_inc(x_free, 1)

            def pair_lo(b, l):
                item = pair_item(l)
                dve.wait_ge(turned_hi, items(b, item))
                nc.vector.scalar_tensor_tensor(out=pt[1][:, (l - 1) % 2].rearrange("p q k c -> p q (k c)"), in0=ps_t[item % 2][:],
                                               scalar=P_SCALE, in1=pt[0][:, (l - 1) % 2].rearrange("p q k c -> p q (k c)"),
                                               op0=ALU.mult, op1=ALU.subtract).then_inc(turned_lo, 1)

            def ctx_lo(b, item):
                dve.wait_ge(turned_hi, items(b, item))
                nc.vector.scalar_tensor_tensor(out=ot[1][:], in0=ps_t[item % 2][:], scalar=1.0 / P_SCALE, in1=ot[0][:],
                                               op0=ALU.mult, op1=ALU.subtract).then_inc(turned_lo, 1)

            def read_context(b, l):
                unit = PAIRS // 4 * b + (l - 6) // 4
                two = (l - 6) // 4 % 2
                dve.wait_ge(pv_done, PAIRS * b + l - 2)
                if not two:
                    wait(dve, turned, items(b, 9 * (l // 8) + 4))
                nc.vector.reciprocal(rsum[:], sums[:, two, :]).then_inc(chain, 1)
                dve.wait_ge(chain, unit + 1)
                nc.vector.tensor_tensor(ctxt[:, :, two * P:two * P + P].rearrange("p t (h d) -> p h t d", h=2),
                                        ps_o[:].rearrange("p (h t d) -> p h t d", h=2, t=TPB),
                                        rsum[:].rearrange("p (h t) -> p h t", h=2).unsqueeze(3).to_broadcast([P, 2, TPB, D]),
                                        ALU.mult).then_inc(ctx_read, 1)

            def combine(b, j):
                for i in range(2):
                    t = 2 * j + i
                    dve.wait_ge(gathered[i], 32 * b + 16 * j + 16)
                    nc.vector.scalar_tensor_tensor(out=yacc[:, t, :], in0=got[:, i, :], scalar=gate[:, t:t + 1],
                                                   in1=yacc[:, t, :], op0=ALU.mult, op1=ALU.add).then_inc(combined, 1)

            def slot(b, l):
                s = PAIRS * b + l
                j, k = divmod(l, 8)
                h = HG * j + k // 2
                if l % 4 == 2 and not (is_first(b) and l == 2):
                    read_context(b, l)
                for q in range(2):
                    start = SW - S - (2 * (l % 2) + q) * P
                    dve.wait_ge(scored, 2 * s + q + 1)
                    wait(dve, exp_done, 2 * s - 3 + q)
                    dve.sem_inc(went_on)
                    i = 2 * (l % 2) + q
                    nc.vector.tensor_tensor_reduce(neg[:, l % 2, q, :], ps_s[q][:], strips[:, h, start:start + S],
                                                   score_scale[:, 0:1], 3.0e38, ALU.add, ALU.min,
                                                   neg_max[:, i:i + 1]).then_inc(negated, 1)
                kind = slot_kind(b, l)
                if kind:
                    read_fill(kind, b, l, fills_before(b, l))
                if l or not is_first(b):
                    pair_lo(b, l)
                if k == 3 and not (is_first(b) and j == 0):
                    ctx_lo(b, 9 * j + 4)
                if l == 13:
                    dve.wait_ge(residual_loaded, 16 * b + 16)
                    combine(b, 0)
                if l == 25:
                    dve.wait_ge(x_free, fills_before(b, 24))
                    combine(b, 1)

            def turn_first(w):
                dve.wait_ge(x_free, 2 * w + 2)
                if w:
                    dve.wait_ge(turned_parts, 6)
                for i, (half, table) in enumerate(((0, cos), (1, sin), (0, sin), (1, cos))):
                    nc.vector.tensor_tensor(prod0[:, i, :], proj0[:, w, half, :], table[:], ALU.mult).then_inc(turned_parts, 1)
                dve.wait_ge(turned_parts, 6 * w + 4)
                nc.vector.tensor_tensor(rot[:, w, 0, :], prod0[:, 0, :], prod0[:, 1, :], ALU.subtract).then_inc(turned_parts, 1)
                nc.vector.tensor_tensor(rot[:, w, 1, :], prod0[:, 2, :], prod0[:, 3, :], ALU.add).then_inc(turned_parts, 1)

            turn_first(0)
            turn_first(1)
            for w in range(2):
                dve.wait_ge(parts_hi, w + 1)
                nc.vector.tensor_tensor(parts[:, 1, w], rot[:, w], parts[:, 0, w], ALU.subtract).then_inc(parts_lo, 1)
            for k in range(2):
                read_fill(("v", k, 0, 0, 0), 0, 0, 0)
            for k in range(2):
                read_fill(("v", k, 0, 1, 1), 0, 0, 0)

            def batch(b):
                for l in range(PAIRS):
                    slot(b, l)

            over_batches(dve, batch)
            pair_lo(NB - 1, PAIRS)
            read_context(NB - 1, PAIRS + 2)
            ctx_lo(NB - 1, 37)
            for k in range(2):
                read_fill(("y", k), NB - 1, 0, fills_before(NB - 1, PAIRS) + k)

        @block.tensor
        def _(pe):
            PARTS = ((0, 0), (0, 1), (1, 0))

            def fill(kind, b, l, fill):
                what, k = kind[:2]
                wait(pe, x_free, fill)
                if what == "qk":
                    g = kind[4]
                    c = k // 2 * H * D + g * HG * D + k % 2 * P
                    m = 0
                    for kt in range(KT):
                        for a, x in PARTS:
                            last = nc.tensor.matmul(ps_x[:], wt[a][:, kt, c:c + P], xcur[:, x, kt, :],
                                                    start=(m == 0), stop=(m == 3 * KT - 1))
                            m += 1
                elif what == "v":
                    c = 2 * H * D + kind[4] * HG * D
                    for i in range(2):
                        t = (2 * k + i) * P
                        m = 0
                        for kt in range(KT):
                            for x, a in PARTS:
                                last = nc.tensor.matmul(ps_x[:, i * M:(i + 1) * M], xcur[:, x, kt, t:t + P],
                                                        wt[a][:, kt, c:c + HG * D], start=(m == 0), stop=(m == 3 * KT - 1))
                                m += 1
                else:
                    g = (l // 8 - 1) % 4
                    for i in range(2):
                        t = (2 * k + i) * P
                        m = 0
                        for kt in range(2):
                            for x, a in PARTS:
                                last = nc.tensor.matmul(ps_x[:, i * M:(i + 1) * M], ot[x][:, kt, t:t + P],
                                                        wot[a][:, 2 * g + kt, :], start=(m == 0), stop=(m == 5))
                                m += 1
                last.then_inc(filled, 1)

            def scores(b, l):
                s = PAIRS * b + l
                j, k = divmod(l, 8)
                if k == 0:
                    pe.wait_ge(qk_moved[j % 2], MOVED * (2 * b + j // 2 + 1))
                for q in range(2):
                    t = (2 * (l % 2) + q) * P
                    wait(pe, negated, 2 * s - 1 + q)
                    nc.tensor.matmul(ps_s[q][:], qk[:, j % 2, 0, k // 2, t:t + P], qk[:, j % 2, 1, k // 2, :], start=True, stop=False)
                    nc.tensor.matmul(ps_s[q][:], qk[:, j % 2, 0, k // 2, t:t + P], kswap[:, j % 2, k // 2, :],
                                     start=False, stop=True).then_inc(scored, 1)

            def transposes(b, l):
                s = PAIRS * b + l
                item = pair_item(l)
                wait(pe, turned_lo, items(b, item - 2))
                for q in range(2):
                    pe.wait_ge(exp_done, 2 * s - 1 + q)
                    for kt in range(TPB):
                        last = nc.tensor.transpose(ps_t[item % 2][:, q, kt * P:(kt + 1) * P],
                                                   prob[:, (l - 1) % 2, q, kt * P:(kt + 1) * P], ident[:])
                last.then_inc(turned, 1)

            def context_transposes(b, item, units):
                wait(pe, turned_lo, items(b, item - 2))
                pe.wait_ge(ctx_read, units)
                for kt in range(2):
                    for t in range(TPB):
                        last = nc.tensor.transpose(ps_t[item % 2][:, kt, t * P:(t + 1) * P],
                                                   ctxt[:, t, kt * P:(kt + 1) * P], ident[:])
                last.then_inc(turned, 1)

            def values(b, l):
                l2 = l - 2
                hd = l2 % 8 // 2 * D
                if l2 % 4 == 0:
                    wait(pe, ctx_read, PAIRS // 4 * b + l2 // 4)
                pe.wait_ge(turned_lo, items(b, pair_item(l - 1)))
                for q in range(2):
                    c = (l2 % 4 // 2 * TPB + 2 * (l2 % 2) + q) * D
                    m = 0
                    for kt in range(TPB):
                        for x, a in PARTS:
                            last = nc.tensor.matmul(ps_o[:, c:c + D], pt[x][:, l % 2, q, kt, :],
                                                    val[a][:, l2 // 8 % 4, kt, hd:hd + D], start=(m == 0), stop=(m == 3 * TPB - 1))
                            m += 1
                last.then_inc(pv_done, 1)

            def slot(b, l):
                j, k = divmod(l, 8)
                scores(b, l)
                kind = slot_kind(b, l)
                if kind:
                    if l == 16 and not is_last(b):
                        pe.wait_ge(x_loaded, 16 * b + 32)
                    if kind[0] == "y" and k == FILLS:
                        pe.wait_ge(turned_lo, items(b, 9 * j + 4))
                    fill(kind, b, l, fills_before(b, l))
                if l or not is_first(b):
                    transposes(b, l)
                if k == 3 and not (is_first(b) and j == 0):
                    context_transposes(b, 9 * j + 4, PAIRS // 4 * b + 2 * j)
                if l >= 2 or not is_first(b):
                    values(b, l)

            pe.wait_ge(x_loaded, 16)
            for n, (F, k) in enumerate(FIRST_FILLS):
                fill(("qk" if k < 4 else "v", k if k < 4 else k - 4, 0, F, F), 0, 0, n)

            def batch(b):
                for l in range(PAIRS):
                    slot(b, l)

            over_batches(pe, batch)
            transposes(NB - 1, PAIRS)
            values(NB - 1, PAIRS)
            values(NB - 1, PAIRS + 1)
            context_transposes(NB - 1, 37, PAIRS // 4 * NB)
            pe.wait_ge(turned_lo, items(NB - 1, 37))
            for k in range(2):
                fill(("y", k), NB - 1, 0, fills_before(NB - 1, PAIRS) + k)


_INS = ['L0_attn_x', 'L0_attn_qkv_w', 'L0_attn_out_w', 'L0_attn_bias_p', 'L0_attn_bias_a', 'L0_attn_rope_freqs',
        'L0_ffn_Wg', 'L0_ffn_w1', 'L0_ffn_w2']
_OUTS = [((8, 512, 256), 'float32')]


def kernel(**inputs):
    import numpy as _np
    import concourse.bacc as _bacc
    from concourse import mybir as _mybir
    from concourse.bass_utils import run_bass_kernel_spmd as _run

    nc = _bacc.Bacc("TRN2", target_bir_lowering=False, num_devices=1)
    arrays, args = {}, []
    for name in _INS:
        a = _np.ascontiguousarray(inputs[name])
        arrays[f"in_{name}_dram"] = a
        args.append(nc.dram_tensor(f"in_{name}_dram", a.shape, _mybir.dt.from_np(a.dtype), kind="ExternalInput").ap())
    for i, (shape, dtype) in enumerate(_OUTS):
        dt = _mybir.dt.from_np(_np.dtype(dtype))
        args.append(nc.dram_tensor(f"out_{i}_dram", shape, dt, kind="ExternalOutput").ap())
    layer(nc, *args)
    r = _run(nc, [arrays], core_ids=[0])
    got = tuple(r.results[0][f"out_{i}_dram"] for i in range(len(_OUTS)))
    return got[0]
```
